# Optimizing a Trainium2 kernel written in Bass

```python
import numpy as np
import jax
import jax.numpy as jnp

def _softmax(x, axis=-1):
    return jax.nn.softmax(x, axis=axis)

def _gelu(x):
    return jax.nn.gelu(x, approximate=True)

def _silu(x):
    return jax.nn.silu(x)

def _sigmoid(x):
    return jax.nn.sigmoid(x)

def _layernorm(x, axis=-1, eps=1e-05):
    m = jnp.mean(x, axis=axis, keepdims=True)
    v = jnp.var(x, axis=axis, keepdims=True)
    return (x - m) / jnp.sqrt(v + eps)

def _scatter_add(tgt, idx, src, axis=0):
    return tgt.at[idx].add(src)

def _segment_sum(src, seg, n):
    return jax.ops.segment_sum(src, seg, n)
kernel_name = 'mk_xattn_ffn_d1_seqx_r8_9c885f'

def setup_inputs(seed: int=0):
    np.random.seed(seed)
    _w = jnp.asarray

    def _rec_inputs():
        import jax
        import jax.numpy as jnp
        _rk = jax.random.key(seed)
        x = 7.22e-05 + 1 * jax.random.normal(jax.random.fold_in(_rk, 1), (128, 64, 128), jnp.float32)
        _lenS = 64 - jax.random.randint(jax.random.fold_in(_rk, 7), (128,), 0, max(1, 64 // 4) + 1, jnp.int32)
        _lenS2 = 64 - jax.random.randint(jax.random.fold_in(_rk, 8), (128,), 0, max(1, 64 // 4) + 1, jnp.int32)
        _ctx_1024P = jax.random.normal(jax.random.fold_in(_rk, 11), (128, 16, 128), jnp.float32)
        _ctx_1024c = jax.random.dirichlet(jax.random.fold_in(_rk, 511), 0.3 * jnp.ones((16,), jnp.float32), (128, 64))
        _ctx_1024t = jnp.einsum('bsk,bkd->bsd', _ctx_1024c, _ctx_1024P)
        _ctx_1024t = _ctx_1024t * jax.lax.rsqrt(jnp.mean(jnp.square(_ctx_1024t)) + 1e-12) * 0.953939
        ctx_1024 = 4.13588e-05 + 0.999923 * (_ctx_1024t + 0.3 * jax.random.normal(jax.random.fold_in(_rk, 611), (128, 64, 128), jnp.float32))
        return (x, ctx_1024)
    x, ctx_1024 = _rec_inputs()

    def _L0_xattn_setup():
        import jax, jax.numpy as jnp
        import numpy as np
        BETA = 128
        NUM_HEADS = 16
        NORM = (BETA // NUM_HEADS) ** (-0.5)
        key = jax.random.key(seed)
        ks = jax.random.split(key, 6)
        B, N = (4, 256)
        D_in_q = D_in_k = D_in_v = 128
        D_out_k = D_out_v = 128
        q = jax.random.normal(ks[0], (B, N, D_in_q), dtype=jnp.float32)
        k = jax.random.normal(ks[1], (B, N, D_in_k), dtype=jnp.float32)
        v = jax.random.normal(ks[2], (B, N, D_in_v), dtype=jnp.float32)
        Wq = jax.random.normal(ks[3], (D_out_k, D_in_q), dtype=jnp.float32) * D_in_q ** (-0.5)
        Wk = jax.random.normal(ks[4], (D_out_k, D_in_k), dtype=jnp.float32) * D_in_k ** (-0.5)
        Wv = jax.random.normal(ks[5], (D_out_v, D_in_v), dtype=jnp.float32) * D_in_v ** (-0.5)
        return {'q': q, 'k': k, 'v': v, 'Wq': Wq, 'Wk': Wk, 'Wv': Wv}
    _L0_xattn_all = _L0_xattn_setup()
    _L0_xattn_in = {k: v for k, v in _L0_xattn_all.items() if k in ('Wq', 'Wk', 'Wv')}
    del _L0_xattn_all

    def _L0_ffn_setup():
        import jax, jax.numpy as jnp
        import numpy as np
        E, TOPK, R = (8, 2, 16)
        D, H, GH = (128, 16, 32)
        HD = D // H
        SCALE = HD ** (-0.5)

        def _svd_moe(x, Wm, U, S, V, b, idx, gates):
            main = jnp.einsum('bsd,od->bso', x, Wm)
            Ug, Sg, Vg = (U[idx], S[idx], V[idx])
            xv = jnp.einsum('bsd,bkrd->bksr', x, Vg)
            xvs = xv * Sg[:, :, None, :]
            eo = jnp.einsum('bksr,bkor->bkso', xvs, Ug)
            expert = jnp.einsum('bkso,bk->bso', eo, gates)
            return main + expert + b
        key = jax.random.key(seed)
        ks = jax.random.split(key, 32)
        B, S = (32, 257)
        inp = {'hidden_states': jax.random.normal(ks[0], (B, S, D), jnp.float32)}
        inp['gw1'] = jax.random.normal(ks[1], (GH, D), jnp.float32) * 0.02
        inp['gb1'] = jnp.zeros((GH,), jnp.float32)
        inp['gw2'] = jax.random.normal(ks[2], (E, GH), jnp.float32) * 0.02
        inp['gb2'] = jnp.zeros((E,), jnp.float32)
        i = 3
        for p in ('q', 'k', 'v', 'o'):
            inp[p + 'Wm'] = jax.random.normal(ks[i], (D, D), jnp.float32) * 0.02
            i += 1
            inp[p + 'U'] = jax.random.normal(ks[i], (E, D, R), jnp.float32) * 0.02
            i += 1
            inp[p + 'S'] = jax.random.normal(ks[i], (E, R), jnp.float32) * 0.1
            i += 1
            inp[p + 'V'] = jax.random.normal(ks[i], (E, R, D), jnp.float32) * 0.02
            i += 1
            inp[p + 'b'] = jnp.zeros((D,), jnp.float32)
        return inp
    _L0_ffn_all = _L0_ffn_setup()
    _L0_ffn_in = {k: v for k, v in _L0_ffn_all.items() if k in ('gw1', 'gb1', 'gw2', 'gb2', 'qWm', 'qU', 'qS', 'qV', 'qb', 'kWm', 'kU', 'kS', 'kV', 'kb', 'vWm', 'vU', 'vS', 'vV', 'vb', 'oWm', 'oU', 'oS', 'oV', 'ob')}
    del _L0_ffn_all
    return {'x': x, 'ctx_1024': ctx_1024, 'L0_xattn_Wq': _L0_xattn_in['Wq'], 'L0_xattn_Wk': _L0_xattn_in['Wk'], 'L0_xattn_Wv': _L0_xattn_in['Wv'], 'L0_ffn_gw1': _L0_ffn_in['gw1'], 'L0_ffn_gb1': _L0_ffn_in['gb1'], 'L0_ffn_gw2': _L0_ffn_in['gw2'], 'L0_ffn_gb2': _L0_ffn_in['gb2'], 'L0_ffn_qWm': _L0_ffn_in['qWm'], 'L0_ffn_qU': _L0_ffn_in['qU'], 'L0_ffn_qS': _L0_ffn_in['qS'], 'L0_ffn_qV': _L0_ffn_in['qV'], 'L0_ffn_qb': _L0_ffn_in['qb'], 'L0_ffn_kWm': _L0_ffn_in['kWm'], 'L0_ffn_kU': _L0_ffn_in['kU'], 'L0_ffn_kS': _L0_ffn_in['kS'], 'L0_ffn_kV': _L0_ffn_in['kV'], 'L0_ffn_kb': _L0_ffn_in['kb'], 'L0_ffn_vWm': _L0_ffn_in['vWm'], 'L0_ffn_vU': _L0_ffn_in['vU'], 'L0_ffn_vS': _L0_ffn_in['vS'], 'L0_ffn_vV': _L0_ffn_in['vV'], 'L0_ffn_vb': _L0_ffn_in['vb'], 'L0_ffn_oWm': _L0_ffn_in['oWm'], 'L0_ffn_oU': _L0_ffn_in['oU'], 'L0_ffn_oS': _L0_ffn_in['oS'], 'L0_ffn_oV': _L0_ffn_in['oV'], 'L0_ffn_ob': _L0_ffn_in['ob']}

def reference(x, ctx_1024, L0_xattn_Wq, L0_xattn_Wk, L0_xattn_Wv, L0_ffn_gw1, L0_ffn_gb1, L0_ffn_gw2, L0_ffn_gb2, L0_ffn_qWm, L0_ffn_qU, L0_ffn_qS, L0_ffn_qV, L0_ffn_qb, L0_ffn_kWm, L0_ffn_kU, L0_ffn_kS, L0_ffn_kV, L0_ffn_kb, L0_ffn_vWm, L0_ffn_vU, L0_ffn_vS, L0_ffn_vV, L0_ffn_vb, L0_ffn_oWm, L0_ffn_oU, L0_ffn_oS, L0_ffn_oV, L0_ffn_ob):
    import jax
    import jax.numpy as jnp

    def _L0_xattn_ref(q, k, v, Wq, Wk, Wv):
        import jax, jax.numpy as jnp
        import numpy as np
        BETA = 128
        NUM_HEADS = 16
        NORM = (BETA // NUM_HEADS) ** (-0.5)
        qp = jax.nn.relu(jnp.einsum('bnd,od->bno', q, Wq))
        kp = jax.nn.relu(jnp.einsum('bnd,od->bno', k, Wk))
        vp = jax.nn.relu(jnp.einsum('bnd,od->bno', v, Wv))
        B, N, D = qp.shape
        dh = D // NUM_HEADS
        qh = qp.reshape(B, N, NUM_HEADS, dh)
        kh = kp.reshape(B, N, NUM_HEADS, dh)
        vh = vp.reshape(B, N, NUM_HEADS, vp.shape[-1] // NUM_HEADS)
        E = NORM * jnp.einsum('bqhd,bkhd->bhqk', qh, kh)
        A = jax.nn.softmax(E, axis=-1)
        out = jnp.einsum('bhqk,bkhd->bqhd', A, vh)
        return out.reshape(B, N, -1)

    def _L0_ffn_ref(hidden_states, gw1, gb1, gw2, gb2, qWm, qU, qS, qV, qb, kWm, kU, kS, kV, kb, vWm, vU, vS, vV, vb, oWm, oU, oS, oV, ob):
        import jax, jax.numpy as jnp
        import numpy as np
        E, TOPK, R = (8, 2, 16)
        D, H, GH = (128, 16, 32)
        HD = D // H
        SCALE = HD ** (-0.5)

        def _svd_moe(x, Wm, U, S, V, b, idx, gates):
            main = jnp.einsum('bsd,od->bso', x, Wm)
            Ug, Sg, Vg = (U[idx], S[idx], V[idx])
            xv = jnp.einsum('bsd,bkrd->bksr', x, Vg)
            xvs = xv * Sg[:, :, None, :]
            eo = jnp.einsum('bksr,bkor->bkso', xvs, Ug)
            expert = jnp.einsum('bkso,bk->bso', eo, gates)
            return main + expert + b
        B, S, _ = hidden_states.shape
        pooled = hidden_states.mean(axis=1)
        h = jax.nn.relu(pooled @ gw1.T + gb1)
        logits = h @ gw2.T + gb2
        top_vals, top_idx = jax.lax.top_k(logits, TOPK)
        gates = jax.nn.softmax(top_vals, axis=-1)
        q = _svd_moe(hidden_states, qWm, qU, qS, qV, qb, top_idx, gates) * SCALE
        k = _svd_moe(hidden_states, kWm, kU, kS, kV, kb, top_idx, gates)
        v = _svd_moe(hidden_states, vWm, vU, vS, vV, vb, top_idx, gates)

        def shp(t):
            return t.reshape(B, S, H, HD).transpose(0, 2, 1, 3)
        q, k, v = (shp(q), shp(k), shp(v))
        attn = jax.nn.softmax(jnp.einsum('bhsd,bhtd->bhst', q, k), axis=-1)
        ctx = jnp.einsum('bhst,bhtd->bhsd', attn, v)
        ctx = ctx.transpose(0, 2, 1, 3).reshape(B, S, D)
        out = _svd_moe(ctx, oWm, oU, oS, oV, ob, top_idx, gates)
        return out
    x = x + _L0_xattn_ref(_layernorm(x, axis=-1), ctx_1024, ctx_1024, L0_xattn_Wq, L0_xattn_Wk, L0_xattn_Wv)
    x = x + _L0_ffn_ref(_layernorm(x, axis=-1), L0_ffn_gw1, L0_ffn_gb1, L0_ffn_gw2, L0_ffn_gb2, L0_ffn_qWm, L0_ffn_qU, L0_ffn_qS, L0_ffn_qV, L0_ffn_qb, L0_ffn_kWm, L0_ffn_kU, L0_ffn_kS, L0_ffn_kV, L0_ffn_kb, L0_ffn_vWm, L0_ffn_vU, L0_ffn_vS, L0_ffn_vV, L0_ffn_vb, L0_ffn_oWm, L0_ffn_oU, L0_ffn_oS, L0_ffn_oV, L0_ffn_ob)
    return x

_drawn_inputs = setup_inputs


def setup_inputs(seed=0):
    import zlib

    import numpy as np

    out = dict(_drawn_inputs(seed))
    spreads = {'L0_ffn_gb1': (0.0, 0.8),
     'L0_ffn_gb2': (0.0, 0.8),
     'L0_ffn_qb': (0.0, 0.8),
     'L0_ffn_kb': (0.0, 0.8),
     'L0_ffn_vb': (0.0, 0.461),
     'L0_ffn_ob': (0.0, 0.1)}
    factors = {'L0_ffn_gw1': 8.0,
     'L0_ffn_gw2': 8.0,
     'L0_ffn_qWm': 8.0,
     'L0_ffn_qU': 8.0,
     'L0_ffn_qS': 8.0,
     'L0_ffn_qV': 8.0,
     'L0_ffn_kWm': 8.0,
     'L0_ffn_kU': 8.0,
     'L0_ffn_kS': 8.0,
     'L0_ffn_kV': 8.0,
     'L0_ffn_vWm': 4.136,
     'L0_ffn_vU': 8.0,
     'L0_ffn_vS': 8.0,
     'L0_ffn_vV': 8.0,
     'L0_ffn_oU': 8.0,
     'L0_ffn_oS': 8.0,
     'L0_ffn_oV': 8.0}
    for name, (base, spread) in spreads.items():
        noise = np.random.default_rng([zlib.crc32(name.encode()), seed]).standard_normal(out[name].shape)
        drawn = base * np.exp(spread * noise) if base else spread * noise
        out[name] = jnp.asarray(drawn.astype(out[name].dtype))
    for name, factor in factors.items():
        out[name] = (out[name] * factor).astype(out[name].dtype)
    return out
```

```python
import concourse.bass as bass
from concourse import mybir
from contextlib import ExitStack


B, S, D = 128, 64, 128
H, DH = 16, 8
E, R, GH = 8, 16, 32
NP = 4
TOK = NP * 2 * S
NC = B // (2 * NP)
EPS = 1e-5
SCALE = DH ** -0.5
PARTS = 3
STACK = 6 * DH
ROWS = 2 * STACK
MROWS = ROWS + 2 * PARTS
VW = DH + 1


class Chunk:

    def __init__(self, layer, it, off):
        self.layer = layer
        self.c = it * 2 + off
        self.n = it * 2 + (off + NC * layer)
        self.k = off % 2
        self.u = it + (off // 2 + NC // 2 * layer)


def after(value):
    return not isinstance(value, int) or value > 0


def xattn_ffn_kernel(nc, x, ctx_in, wq, wk, wv, gw1, gb1, gw2, gb2,
                     qWm, qU, qS, qV, qb, kWm, kU, kS, kV, kb,
                     vWm, vU, vS, vV, vb, oWm, oU, oS, oV, ob, out):
    f32, bf16 = mybir.dt.float32, mybir.dt.bfloat16
    ALU, ACT, AX = mybir.AluOpType, mybir.ActivationFunctionType, mybir.AxisListType

    x_d = x.rearrange("(p b) t f -> (b t) p f", b=2)
    c_d = ctx_in.rearrange("(p b) t f -> (b t) p f", b=2)
    o_d = out.rearrange("(p b) t f -> (b t) p f", b=2)

    qpd = [nc.dram_tensor(f"q_parts_dram{k}", [PARTS, DH, H, TOK], bf16, kind="Internal").ap() for k in range(2)]
    kpd = [nc.dram_tensor(f"k_parts_dram{k}", [PARTS, DH, H, TOK], bf16, kind="Internal").ap() for k in range(2)]
    mxd = [nc.dram_tensor(f"max_dram{k}", [2, PARTS, H // 2, 2, NP, S], bf16, kind="Internal").ap() for k in range(2)]

    NAMES = ["wq", "wk", "wv", "qW", "kW", "vW", "oW", "qV", "kV", "vV", "oV", "qU", "kU", "vU", "oU"]
    NW = len(NAMES)
    SCALED = ("wq", "qW", "qU")
    WI = {n: i for i, n in enumerate(NAMES)}
    w_src = dict(wq=wq, wk=wk, wv=wv, qW=qWm, kW=kWm, vW=vWm, oW=oWm)
    for n, v in (("qV", qV), ("kV", kV), ("vV", vV), ("oV", oV)):
        w_src[n] = v.rearrange("e r d -> (e r) d")
    u_src = dict(qU=qU, kU=kU, vU=vU, oU=oU)

    with ExitStack() as st:
        def sb(name, shape, dt=f32):
            return st.enter_context(nc.sbuf_tensor(name, shape, dt))

        def sem(name):
            return st.enter_context(nc.semaphore(name))

        def sem2(name):
            return [sem(f"{name}{k}") for k in range(2)]

        x1 = sb("x1", [128, NC * NP, D])
        zT = sb("zT", [128, NC * TOK])
        kbd = [sb(f"kbd{k}", [MROWS, H, 2 * S, NP], bf16) for k in range(2)]
        qst = [sb(f"qst{k}", [MROWS, H, NP, S], bf16) for k in range(2)]
        w_nat = zT[:, 0:NW * D].rearrange("p (n f) -> p n f", n=NW)
        ones3 = zT[0:PARTS, 2048:2048 + H * S * NP // 2].bitcast(bf16)
        prob = [sb(f"prob{j}", [128, 8, S]) for j in range(4)]
        vbd = [sb(f"vbd{k}", [128, NP, H, 2 * VW]) for k in range(2)]
        wT = sb("wT", [128, NW, D])
        ident = sb("ident", [128, 128])
        identb = sb("identb", [128, 128], bf16)
        ctx_sb = [sb(f"ctx_sb{k}", [128, NP, D]) for k in range(2)]
        xn = [sb(f"xn{k}", [128, NP, D]) for k in range(2)]
        z = sb("z", [128, NP, D])
        fT = sb("fT", [128, TOK])
        cT = sb("cT", [128, TOK])
        qpart = [sb(f"qpart{k}", [128, PARTS, TOK], bf16) for k in range(2)]
        kpart = [sb(f"kpart{k}", [128, PARTS, TOK], bf16) for k in range(2)]
        q_rest = sb("q_rest", [128, TOK])
        k_rest = sb("k_rest", [128, TOK])
        mx = sb("mx", [128, 2, H // 2, NP])
        mxp = sb("mxp", [128, 2, PARTS, H // 2, NP], bf16)
        mx_rest = sb("mx_rest", [128, 2, H // 2, NP])
        mxT = [sb(f"mxT{k}", [PARTS * 8 * NP, 2, 128], bf16) for k in range(2)]
        av_sb = [sb(f"av_sb{j}", [128, 256]) for j in range(2)]
        rden = sb("rden", [128, 2, 8, 2])
        att = sb("att", [128, NP, D])
        stats = sb("stats", [128, NP, 6])
        mv = sb("mv", [128, NP, 2])
        rstd = sb("rstd", [128, NP])
        m_half = sb("m_half", [128, NP])
        eps_c = sb("eps_c", [128, NP])
        stats2 = sb("stats2", [128, NP, 6])
        mv2 = sb("mv2", [128, NP, 2])
        rstd2 = sb("rstd2", [128, NP])
        xvs = {p: sb("xvs_" + p, [128, TOK]) for p in "vo"}
        for k, p in enumerate("qk"):
            xvs[p] = xn[k][:].rearrange("e p f -> e (p f)")
        attT, xo, osb = fT, z, ctx_sb
        vb_bc = sb("vb_bc", [128, D])
        ob_bc = sb("ob_bc", [128, D])
        qb_c = sb("qb_c", [128, 1])
        qbs_c = sb("qbs_c", [128, 1])
        kb_c = sb("kb_c", [128, 1])
        s_col = sb("s_col", [128, 4])
        gw1_nat = sb("gw1_nat", [GH, D])
        gw1T = sb("gw1T", [128, GH])
        gb1_c = sb("gb1_c", [GH, 1])
        gw2T = sb("gw2T", [GH + 1, E])
        hid = sb("hid", [GH + 1, B])
        pooled = sb("pooled", [128, B])
        lg = sb("lg", [128, E])
        tri = sb("tri", [128, E, E])
        beat = sb("beat", [128, E, E])
        tie = sb("tie", [128, E, E])
        rank = sb("rank", [128, E])
        nmax = sb("nmax", [128, 1])
        ex = sb("ex", [128, E])
        gsum = sb("gsum", [128, 1])
        rsum = sb("rsum", [128, 1])
        gexp = sb("gexp", [128, E, R])
        sg = {p: sb("sg_" + p, [128, B]) for p in "qkvo"}

        def pb(name):
            return st.enter_context(nc.psum_tensor(name, [128, 512], f32))
        s1 = [pb(f"ps_s1_{j}") for j in range(2)]
        s2 = [pb(f"ps_s2_{j}") for j in range(2)]
        av = [pb(f"ps_av_{j}") for j in range(2)]
        pa = [pb(f"ps_a_{j}") for j in range(2)]
        mT_ps = s1[0][:, 0:128].bitcast(bf16).rearrange("p (b c) -> p b c", b=2)

        d_w = sem("d_w")
        d_ones = sem("d_ones")
        d_x, d_ctx = sem2("d_x"), sem2("d_ctx")
        d_qput, d_kput = sem2("d_qput"), sem2("d_kput")
        d_qget, d_kget = sem2("d_qget"), sem2("d_kget")
        d_mput, d_mget = sem2("d_mput"), sem2("d_mget")
        d_out = sem2("d_out")
        c_set = sem("c_set")
        c_zero = sem("c_zero")
        w_ps, w_done = sem("w_ps"), sem("w_done")
        ln_mv, ln_rs, ln_x = sem("ln_mv"), sem("ln_rs"), sem("ln_x")
        l2_mv, l2_rs, l2_z = sem("l2_mv"), sem("l2_rs"), sem("l2_z")
        xT_ps, xT_ok, cT_ps, cT_ok = sem("xT_ps"), sem("xT_ok"), sem("cT_ps"), sem("cT_ok")
        ln_ve, l2_ve = sem("ln_ve"), sem("l2_ve")
        zT_ps, zT_ok, pool_ok = sem("zT_ps"), sem("zT_ok"), sem("pool_ok")
        q_ps, q_hi, q_r, q_mid, q_lo = sem("q_ps"), sem("q_hi"), sem("q_r"), sem("q_mid"), sem("q_lo")
        k_ps, k_hi, k_r, k_mid, k_lo = sem("k_ps"), sem("k_hi"), sem("k_r"), sem("k_mid"), sem("k_lo")
        v_ps, v_ok = sem("v_ps"), sem("v_ok")
        sc_ps, max_ok = sem("sc_ps"), sem("max_ok")
        m_hi, m_r, m_mid, m_parts = sem("m_hi"), sem("m_r"), sem("m_mid"), sem("m_parts")
        mT_pe, mT_ok = sem("mT_pe"), sem("mT_ok")
        s2_ps, exp_ok, av_ps, av_ok, avT_ps = sem("s2_ps"), sem("exp_ok"), sem("av_ps"), sem("av_ok"), sem("avT_ps")
        rden_ok, att_ok, add_ok = sem("rden_ok"), sem("att_ok"), sem("add_ok")
        xv_ps = {p: sem("xv_ps_" + p) for p in "qkvo"}
        xv_ok = {p: sem("xv_ok_" + p) for p in "qkvo"}
        f_ok = sem("f_ok")
        aT_ps, aT_ok, o_ps, o_ok, xo_ok = sem("aT_ps"), sem("aT_ok"), sem("o_ps"), sem("o_ok"), sem("xo_ok")
        g_pe, g_act, g_dve = sem("g_pe"), sem("g_act"), sem("g_dve")

        block = st.enter_context(nc.Block())
        N_W_DMA = NW + 14

        def walk(eng, layer, first, step, last):
            ch = lambda it, off: Chunk(layer, it, off)
            first(ch)
            for i in range(2):
                step(ch(0, i + 2), ch(0, i + 1), ch(0, i), ch(0, i - 1) if i else None, ch(0, i + 3))
            looped = (NC - 4, NC - 2)[layer]
            with eng.Fori(1, looped // 2) as it:
                for k in range(2):
                    step(ch(it, k + 2), ch(it, k + 1), ch(it, k), ch(it, k - 1), ch(it, k + 3) if layer == 0 else None)
            for i in range(looped, NC):
                prep, mxc, ahead = (ch(0, i + j) if i + j < NC else None for j in (2, 1, 3))
                step(prep, mxc, ch(0, i), ch(0, i - 1), ahead)
            last(ch(0, NC - 1))

        @block.sync
        def _(sp):
            for n, name in enumerate(NAMES):
                if name in w_src:
                    sp.dma_start(w_nat[:, n, :], w_src[name]).then_inc(d_w, 16)
                else:
                    sp.dma_start(w_nat[:, n, :].rearrange("o (e r) -> o e r", e=E),
                                 u_src[name].rearrange("e o r -> o e r")).then_inc(d_w, 16)
            sp.dma_start(vb_bc[:], vb[None, :].broadcast_to([128, D])).then_inc(d_w, 16)
            sp.dma_start(ob_bc[:], ob[None, :].broadcast_to([128, D])).then_inc(d_w, 16)
            sp.dma_start(qb_c[:], qb[:, None]).then_inc(d_w, 16)
            sp.dma_start(kb_c[:], kb[:, None]).then_inc(d_w, 16)
            for j, s_ in enumerate((qS, kS, vS, oS)):
                sp.dma_start(s_col[:, j:j + 1], s_.rearrange("e r -> (e r)")[:, None]).then_inc(d_w, 16)
            sp.dma_start(gw1_nat[:], gw1).then_inc(d_w, 16)
            sp.dma_start(gb1_c[:], gb1[:, None]).then_inc(d_w, 16)
            sp.dma_start(gw2T[0:GH, :], gw2.rearrange("e g -> g e"), allow_slow_non_contiguous=True).then_inc(d_w, 16)
            sp.dma_start(gw2T[GH:GH + 1, :], gb2[None, :]).then_inc(d_w, 16)
            sp.wait_ge(c_zero, 4)
            for k in range(2):
                for b in range(2):
                    r = ROWS + PARTS * b
                    sp.dma_start(kbd[k][r:r + PARTS, :, S * b:S * b + S, :],
                                 ones3[:].rearrange("r (h t p) -> r h t p", h=H, p=NP)).then_inc(d_ones, 16)

            def held(*values):
                return [v if isinstance(v, int) else sp.snap(sp.to_reg(v)) for v in values]

            def load(c):
                came, turned = held(c.u * 16, c.n - 1)
                if after(came):
                    sp.wait_ge(d_x[c.k], came)
                sp.dma_start(x1[:, bass.ds(c.c * NP, NP), :], x_d[:, bass.ds(c.c * NP, NP), :]).then_inc(d_x[c.k], 16)
                if after(turned):
                    sp.wait_ge(cT_ps, turned)
                sp.dma_start(ctx_sb[c.k][:], c_d[:, bass.ds(c.c * NP, NP), :]).then_inc(d_ctx[c.k], 16)

            def put(c):
                cut, read = held(c.n + 1, c.u * 96)
                for lo, got, src, dst, done in ((q_lo, d_qget, qpart, qpd, d_qput), (k_lo, d_kget, kpart, kpd, d_kput)):
                    sp.wait_ge(lo, cut)
                    if after(read):
                        sp.wait_ge(got[c.k], read)
                    for s in range(PARTS):
                        sp.dma_start(dst[c.k][s].rearrange("d h t -> h d t"), src[c.k][:, s, :]).then_inc(done[c.k], 16)

            def get(c):
                freed, stored = held((c.n - 1) * 8, c.u * 48 + 48)
                if after(freed):
                    sp.wait_ge(s2_ps, freed)
                sp.wait_ge(d_kput[c.k], stored)
                sp.wait_ge(d_qput[c.k], stored)
                kr = kpd[c.k].rearrange("s d h t -> (s d) h t")
                qr = qpd[c.k].rearrange("s d h t -> (s d) h t")
                for b in range(2):
                    r, t = STACK * b, TOK // 2 * b
                    for at, n, ksrc in ((0, 24, 0), (24, 16, 8), (40, 8, 16)):
                        sp.dma_start(kbd[c.k][r + at:r + at + n, :, S * b:S * b + S, :].rearrange("r h t p -> r h (t p)"),
                                     kr[ksrc:ksrc + n, :, t:t + TOK // 2]).then_inc(d_kget[c.k], 16)
                        sp.dma_start(qst[c.k][r + at:r + at + n, :, :, :].rearrange("r h p t -> r h (p t)"),
                                     qr[0:n, :, t:t + TOK // 2]).then_inc(d_qget[c.k], 16)

            def maxima(c):
                turned, got, stored, freed = held(c.n + 1, c.u * 16, c.u * 64 + 64, (c.n - 1) * 8)
                sp.wait_ge(mT_ok, turned)
                if after(got):
                    sp.wait_ge(d_mget[c.k], got)
                for b in range(2):
                    for a in range(2):
                        sp.dma_start(mxd[c.k][b, :, :, a].rearrange("s g p t -> (s g) p t"),
                                     mxT[c.k][:, b, S * a:S * a + S]).then_inc(d_mput[c.k], 16)
                sp.wait_ge(d_mput[c.k], stored)
                if after(freed):
                    sp.wait_ge(s2_ps, freed)
                sp.dma_start(qst[c.k][ROWS:MROWS, :, :, :].rearrange("r h p t -> r (h p t)"),
                             mxd[c.k].rearrange("b s g a p t -> (b s) (g a p t)")).then_inc(d_mget[c.k], 16)

            for layer in range(2):
                def first(ch):
                    if layer == 0:
                        for j in range(3):
                            load(ch(0, j))
                    for j in range(2):
                        put(ch(0, j))
                        get(ch(0, j))
                    maxima(ch(0, 0))

                def step(prep, mxc, att_c, done, ahead):
                    if layer == 0 and ahead is not None:
                        load(ahead)
                    if layer == 1 and done is not None:
                        store(done)
                    if prep is not None:
                        put(prep)
                    if mxc is not None:
                        maxima(mxc)
                    if prep is not None:
                        get(prep)

                def store(c):
                    ready, at = held(c.c + 1, c.c * NP)
                    sp.wait_ge(o_ok, ready)
                    sp.dma_start(o_d[:, bass.ds(at, NP), :], osb[c.k][:]).then_inc(d_out[c.k], 16)
                walk(sp, layer, first, step, store if layer == 1 else (lambda c: None))
            for k in range(2):
                sp.wait_ge(d_out[k], 16 * NC // 2)

        @block.gpsimd
        def _(pool):
            nc.gpsimd.memset(ident[:], 0.0).then_inc(c_set, 1)
            nc.gpsimd.memset(tri[:], 1.0).then_inc(c_set, 1)
            pool.wait_ge(c_set, 2)
            nc.gpsimd.affine_select(out=ident[:], in_=ident[:], compare_op=ALU.not_equal, fill=1.0, base=0,
                                    pattern=[[-1, 128]], channel_multiplier=1).then_inc(c_set, 1)
            nc.gpsimd.affine_select(out=tri[:], in_=tri[:], compare_op=ALU.is_ge, fill=0.0, base=-1,
                                    pattern=[[1, E], [-1, E]], channel_multiplier=0).then_inc(c_set, 1)
            pool.wait_ge(c_set, 4)
            nc.gpsimd.tensor_copy(identb[:], ident[:]).then_inc(c_set, 1)
            nc.gpsimd.memset(m_half[:], -0.5).then_inc(c_set, 1)
            nc.gpsimd.memset(eps_c[:], EPS).then_inc(c_set, 1)
            pool.wait_ge(c_set, 7)

            def low_parts(c):
                for mid, rest, part, order, putd, lo in ((q_mid, q_rest, qpart, (1, 2), d_qput, q_lo),
                                                         (k_mid, k_rest, kpart, (1, 0), d_kput, k_lo)):
                    pool.wait_ge(mid, c.n + 1)
                    nc.gpsimd.tensor_tensor(part[c.k][:, order[1], :], rest[:], part[c.k][:, order[0], :],
                                            ALU.subtract).then_inc(lo, 1)

            def ahead_rstd(c):
                pool.wait_ge(ln_mv, c.c * NP + NP)
                nc.gpsimd.tensor_tensor(rstd[:], mv[:, :, 1], eps_c[:], ALU.add).then_inc(ln_ve, 1)
                pool.wait_ge(ln_ve, c.c + 1)
                nc.gpsimd.tensor_tensor(rstd[:], rstd[:], m_half[:], ALU.pow).then_inc(ln_rs, 1)

            def result_rstd(c):
                pool.wait_ge(l2_mv, c.c * NP + NP)
                nc.gpsimd.tensor_tensor(rstd2[:], mv2[:, :, 1], eps_c[:], ALU.add).then_inc(l2_ve, 1)
                pool.wait_ge(l2_ve, c.c + 1)
                nc.gpsimd.tensor_tensor(rstd2[:], rstd2[:], m_half[:], ALU.pow).then_inc(l2_rs, 1)

            def residual(c, pairs):
                for p in pairs:
                    pool.wait_ge(att_ok, c.n * NP + (p + 1))
                    xp = x1[:, bass.ds(c.c * NP + p, 1), :]
                    nc.gpsimd.tensor_tensor(xp, xp, att[:, p:p + 1, :], ALU.add).then_inc(add_ok, 1)

            def fetch(c):
                if c.layer == 1:
                    if after(c.c):
                        pool.wait_ge(v_ps, c.n)
                    pool.wait_ge(zT_ok, NC)
                    nc.gpsimd.tensor_copy(cT[:], zT[:, bass.ds(c.c * TOK, TOK)]).then_inc(f_ok, 1)

            for layer in range(2):
                def first(ch):
                    if layer == 0:
                        ahead_rstd(ch(0, 0))
                        ahead_rstd(ch(0, 1))
                    for j in range(2):
                        fetch(ch(0, j))
                        low_parts(ch(0, j))
                    if layer == 0:
                        ahead_rstd(ch(0, 2))

                def step(prep, mxc, att_c, done, ahead):
                    if layer == 1 and done is not None:
                        if after(done.c):
                            pool.wait_ge(o_ok, done.c)
                        nc.gpsimd.tensor_tensor(xo[:], x1[:, bass.ds(done.c * NP, NP), :],
                                                ob_bc[:, None, :].broadcast_to([128, NP, D]), ALU.add).then_inc(xo_ok, 1)
                    if layer == 0 and done is not None:
                        result_rstd(done)
                    if prep is not None:
                        fetch(prep)
                        low_parts(prep)
                    if layer == 0 and att_c is not None:
                        residual(att_c, (0, 1))
                        if ahead is not None:
                            ahead_rstd(ahead)
                        residual(att_c, (2, 3))
                walk(pool, layer, first, step, lambda c: step(None, None, None, c, None))

        @block.scalar
        def _(act):
            for n in range(NW):
                act.wait_ge(w_ps, n + 1)
                nc.scalar.activation(wT[:, n, :], pa[n % 2][:, 0:128], ACT.Copy,
                                     scale=SCALE if NAMES[n] in SCALED else 1.0).then_inc(w_done, 1)
            act.wait_ge(w_ps, NW + 1)
            nc.scalar.activation(gw1T[:], pa[NW % 2][:, 0:GH], ACT.Copy, scale=1.0 / S).then_inc(w_done, 1)
            nc.scalar.mul(qbs_c[:], qb_c[:], SCALE).then_inc(w_done, 1)

            def fill(c, done):
                if c is not None and c.layer == 0:
                    act.wait_ge(xT_ps, c.n + 1)
                    nc.scalar.copy(fT[:], pa[0][:]).then_inc(xT_ok, 1)
                    act.wait_ge(cT_ps, c.n + 1)
                    nc.scalar.copy(cT[:], pa[1][:]).then_inc(cT_ok, 1)
                if done is not None and done.layer == 1:
                    act.wait_ge(aT_ps, done.c + 1)
                    nc.scalar.copy(attT[:], pa[0][:]).then_inc(aT_ok, 1)
                if c is not None:
                    func = ACT.Relu if c.layer == 0 else ACT.Identity
                    act.wait_ge(q_ps, c.n + 1)
                    if after(c.u * 48):
                        act.wait_ge(d_qput[c.k], c.u * 48)
                    nc.scalar.activation(qpart[c.k][:, 0, :].rearrange("f (b p t) -> f p b t", b=2, p=NP),
                                         (pa[0] if c.layer == 0 else pa[1])[:].rearrange("f (p b t) -> f p b t", p=NP, b=2), func,
                                         bias=qbs_c[:] if c.layer else 0.0).then_inc(q_hi, 1)
                    act.wait_ge(k_ps, c.n + 1)
                    if after(c.u * 48):
                        act.wait_ge(d_kput[c.k], c.u * 48)
                    nc.scalar.activation(kpart[c.k][:, 2, :].rearrange("f (b t p) -> f p b t", b=2, p=NP),
                                         pa[1][:].rearrange("f (p b t) -> f p b t", p=NP, b=2), func,
                                         bias=kb_c[:] if c.layer else 0.0).then_inc(k_hi, 1)
                if done is not None and done.layer == 0:
                    act.wait_ge(zT_ps, done.c + 1)
                    nc.scalar.copy(zT[:, bass.ds(done.c * TOK, TOK)], pa[1][:]).then_inc(zT_ok, 1)

            def values(c):
                if c.layer == 0:
                    act.wait_ge(v_ps, c.n + 1)
                    if after((c.n - 1) * 8):
                        act.wait_ge(av_ps, (c.n - 1) * 8)
                    for b in range(2):
                        last = nc.scalar.activation(
                            vbd[c.k][S * b:S * b + S, :, :, VW * b:VW * b + DH].rearrange("t p h d -> t (p h) d"),
                            pa[0][S * b:S * b + S, :].rearrange("t (p d) -> t p d", d=DH), ACT.Relu)
                    last.then_inc(v_ok, 1)

            def maxT(c):
                act.wait_ge(mT_pe, c.n + 1)
                if after(c.u * 64):
                    act.wait_ge(d_mput[c.k], c.u * 64)
                nc.scalar.copy(mxT[c.k][:], mT_ps[0:96]).then_inc(mT_ok, 1)

            for layer in range(2):
                def first(ch):
                    for j in range(2):
                        fill(ch(0, j), None)
                        values(ch(0, j))
                    maxT(ch(0, 0))

                def step(prep, mxc, att_c, done, ahead):
                    fill(prep, done)
                    g = att_c.n * 8
                    for n in range(9):
                        if n < 8:
                            act.wait_ge(s2_ps, g + (n + 1))
                            if after(g + (n - 3)):
                                act.wait_ge(av_ps, g + (n - 3))
                            nc.scalar.activation(prob[n % 4][:].rearrange("p h t -> p (h t)"), s2[n % 2][:],
                                                 ACT.Exp).then_inc(exp_ok, 1)
                        if n >= 2 and n % 2 == 0:
                            p = n // 2 - 1
                            act.wait_ge(av_ps, g + (2 * p + 2))
                            if after(att_c.n * NP + (p - 1)):
                                act.wait_ge(avT_ps, att_c.n * NP + (p - 1))
                            nc.scalar.copy(av_sb[p % 2][:], av[p % 2][:, 0:256]).then_inc(av_ok, 1)
                        if n == 5 and mxc is not None:
                            maxT(mxc)
                    if prep is not None:
                        values(prep)

                walk(act, layer, first, step, lambda c: fill(None, c))
                if layer == 0:
                    act.wait_ge(g_pe, 1)
                    nc.scalar.activation(hid[0:GH, :], s1[0][0:GH, 0:B], ACT.Relu, bias=gb1_c[:]).then_inc(g_act, 1)
                    act.wait_ge(g_dve, 4)
                    nc.scalar.activation(ex[:], lg[:], ACT.Exp, bias=nmax[:]).then_inc(g_act, 1)

        @block.vector
        def _(dve):
            for k in range(2):
                nc.vector.memset(kbd[k][:].rearrange("r h t p -> r (h t p)").bitcast(f32), 0.0).then_inc(c_zero, 1)
            nc.vector.memset(ones3[:], 1.0).then_inc(c_zero, 1)
            nc.vector.memset(pooled[:], 0.0).then_inc(c_zero, 1)
            for k in range(2):
                nc.vector.memset(vbd[k][:], 0.0).then_inc(c_zero, 1)
                nc.vector.memset(av[k][:], 0.0).then_inc(c_zero, 1)
            dve.wait_ge(c_zero, 8)
            for k in range(2):
                for b in range(2):
                    nc.vector.memset(vbd[k][S * b:S * b + S, :, :, VW * b + DH:VW * b + VW], 1.0).then_inc(c_zero, 1)

            nc.vector.memset(hid[GH:GH + 1, :], 1.0).then_inc(c_zero, 1)

            def norm_ahead(c):
                dve.wait_ge(d_x[c.k], c.u * 16 + 16)
                xc = x1[:, bass.ds(c.c * NP, NP), :]
                for p in range(NP):
                    nc.vector.bn_stats(stats[:, p, :], x1[:, bass.ds(c.c * NP + p, 1), :])
                dve.drain()
                for p in range(NP):
                    nc.vector.bn_aggr(mv[:, p, :], stats[:, p, :]).then_inc(ln_mv, 1)
                dve.wait_ge(ln_rs, c.c + 1)
                if after(c.c - 1):
                    dve.wait_ge(xT_ps, c.c - 1)
                for p in range(NP):
                    nc.vector.tensor_scalar(xn[c.k][:, p:p + 1, :], x1[:, bass.ds(c.c * NP + p, 1), :], mv[:, p, 0:1], rstd[:, p:p + 1],
                                            ALU.subtract, ALU.mult).then_inc(ln_x, 1)

            def norm_result(c):
                dve.wait_ge(add_ok, c.c * NP + NP)
                for p in range(NP):
                    nc.vector.bn_stats(stats2[:, p, :], x1[:, bass.ds(c.c * NP + p, 1), :])
                dve.drain()
                for p in range(NP):
                    nc.vector.bn_aggr(mv2[:, p, :], stats2[:, p, :]).then_inc(l2_mv, 1)
                dve.wait_ge(l2_rs, c.c + 1)
                if after(c.c):
                    dve.wait_ge(zT_ps, c.c)
                for p in range(NP):
                    nc.vector.tensor_scalar(z[:, p:p + 1, :], x1[:, bass.ds(c.c * NP + p, 1), :], mv2[:, p, 0:1], rstd2[:, p:p + 1],
                                            ALU.subtract, ALU.mult).then_inc(l2_z, 1)

            def pool_tokens(c):
                dve.wait_ge(zT_ok, c.c + 1)
                nc.vector.tensor_reduce(pooled[:, bass.ds(c.c * 2 * NP, 2 * NP)],
                                        zT[:, bass.ds(c.c * TOK, TOK)].rearrange("f (b t) -> f b t", t=S),
                                        AX.X, ALU.add).then_inc(pool_ok, 1)

            def rest(c, which):
                if which == "q":
                    ps, hi, rs, mids, lo = pa[0] if c.layer == 0 else pa[1], q_hi, q_r, q_mid, q_lo
                    part, dst, order, bias, view = qpart, q_rest, (0, 1), qbs_c, "f (b p t) -> f p b t"
                else:
                    ps, hi, rs, mids, lo = pa[1], k_hi, k_r, k_mid, k_lo
                    part, dst, order, bias, view = kpart, k_rest, (2, 1), kb_c, "f (b t p) -> f p b t"
                dve.wait_ge(hi, c.n + 1)
                if after(c.n):
                    dve.wait_ge(lo, c.n)
                for b in range(2):
                    last = nc.vector.scalar_tensor_tensor(out=dst[:].rearrange(view, b=2, p=NP)[:, :, b],
                                                          in0=ps[:].rearrange("f (p b t) -> f p b t", p=NP, b=2)[:, :, b],
                                                          scalar=bias[:] if c.layer else 0.0,
                                                          in1=part[c.k][:, order[0], :].rearrange(view, b=2, p=NP)[:, :, b],
                                                          op0=ALU.add if c.layer else ALU.max, op1=ALU.subtract)
                last.then_inc(rs, 1)
                dve.wait_ge(rs, c.n + 1)
                nc.vector.tensor_copy(part[c.k][:, order[1], :], dst[:]).then_inc(mids, 1)

            def gate_rank(c, p, bank):
                dve.wait_ge(xv_ps[p], c.c + 1)
                if p == "v" or p == "q" or p == "k":
                    used = {"q": q_ps, "k": k_ps, "v": v_ps}[p]
                    if after(c.c):
                        dve.wait_ge(used, c.n)
                elif after(c.c):
                    dve.wait_ge(o_ps, c.c)
                nc.vector.tensor_tensor(xvs[p][:].rearrange("e (b t) -> e b t", t=S), bank[:].rearrange("e (b t) -> e b t", t=S),
                                        sg[p][:, bass.ds(c.c * 2 * NP, 2 * NP)].rearrange("e (b o) -> e b o", o=1).broadcast_to([128, 2 * NP, S]),
                                        ALU.mult).then_inc(xv_ok[p], 1)

            def maxima(c, unit):
                p, g = unit // 2, unit % 2
                dve.wait_ge(sc_ps, c.n * 8 + (unit + 1))
                nc.vector.tensor_reduce(mx[:, :, 4 * g:4 * g + 4, p].rearrange("q b g -> q g b"),
                                        s1[unit % 2][:].rearrange("q (g b k) -> q g b k", g=4, b=2),
                                        AX.X, ALU.max).then_inc(max_ok, 1)

            def max_parts(c):
                dve.wait_ge(max_ok, c.n * 8 + 8)
                if after(c.n):
                    dve.wait_ge(mT_pe, c.n)
                nc.vector.tensor_scalar(mxp[:, :, 0], mx[:], -1.0, None, ALU.mult).then_inc(m_hi, 1)
                dve.wait_ge(m_hi, c.n + 1)
                nc.vector.scalar_tensor_tensor(out=mx_rest[:], in0=mx[:], scalar=-1.0, in1=mxp[:, :, 0],
                                               op0=ALU.mult, op1=ALU.subtract).then_inc(m_r, 1)
                dve.wait_ge(m_r, c.n + 1)
                nc.vector.tensor_copy(mxp[:, :, 1], mx_rest[:]).then_inc(m_mid, 1)
                dve.wait_ge(m_mid, c.n + 1)
                nc.vector.tensor_tensor(mxp[:, :, 2], mx_rest[:], mxp[:, :, 1], ALU.subtract).then_inc(m_parts, 1)

            def divide(c, p):
                j = c.n * NP + (p + 1)
                dve.wait_ge(avT_ps, j)
                vw = av[p % 2][:, 256:512].rearrange("q (g w) -> q g w", w=32)
                nc.vector.reciprocal(rden[:, p % 2], vw[:, :, DH:2 * VW:VW]).then_inc(rden_ok, 1)
                dve.wait_ge(rden_ok, j)
                if c.layer == 0 and after(c.n * NP + (p - NP + 1)):
                    dve.wait_ge(add_ok, c.n * NP + (p - NP + 1))
                if c.layer == 1 and after(c.c):
                    dve.wait_ge(aT_ps, c.c)
                for hp in range(2):
                    for b in range(2):
                        q0 = S * hp
                        last = nc.vector.tensor_tensor(
                            att[S * b:S * b + S, p, :].rearrange("q (s e c d) -> q s e c d", s=2, e=2, c=4)[:, :, hp],
                            vw[q0:q0 + S, :, VW * b:VW * b + DH].rearrange("q (s c) d -> q s c d", s=2),
                            rden[q0:q0 + S, p % 2, :, b:b + 1].rearrange("q (s c) o -> q s c o", s=2).broadcast_to([S, 2, 4, DH]), ALU.mult)
                last.then_inc(att_ok, 1)

            def values(c):
                if c.layer == 1:
                    dve.wait_ge(v_ps, c.n + 1)
                    if after((c.n - 1) * 8):
                        dve.wait_ge(av_ps, (c.n - 1) * 8)
                    for b in range(2):
                        last = nc.vector.tensor_tensor(
                            vbd[c.k][S * b:S * b + S, :, :, VW * b:VW * b + DH],
                            pa[0][S * b:S * b + S, :].rearrange("t (p h d) -> t p h d", p=NP, h=H),
                            vb_bc[S * b:S * b + S, :].rearrange("t (o h d) -> t o h d", o=1, h=H).broadcast_to([S, NP, H, DH]), ALU.add)
                    last.then_inc(v_ok, 1)

            def fill(c, done):
                if c is not None and c.layer == 1:
                    gate_rank(c, "q", pa[1])
                if done is not None and done.layer == 1:
                    gate_rank(done, "o", pa[0])
                if done is not None and done.layer == 0:
                    norm_result(done)
                if c is not None:
                    rest(c, "q")
                if done is not None and done.layer == 1:
                    dve.wait_ge(o_ps, done.c + 1)
                    dve.wait_ge(xo_ok, done.c + 1)
                    if after((done.c - 1)):
                        dve.wait_ge(d_out[done.k], (done.u - NC // 2) * 16)
                    nc.vector.tensor_tensor(osb[done.k][:].rearrange("t p f -> t (p f)"), pa[0][:],
                                            xo[:].rearrange("t p f -> t (p f)"), ALU.add).then_inc(o_ok, 1)
                if c is not None and c.layer == 1:
                    gate_rank(c, "k", pa[1])
                    gate_rank(c, "v", pa[0])
                if c is not None:
                    rest(c, "k")

            for layer in range(2):
                def first(ch):
                    if layer == 0:
                        for j in range(3):
                            if j < 2:
                                norm_ahead(ch(0, j))
                    for j in range(2):
                        fill(ch(0, j), None)
                        values(ch(0, j))
                    if layer == 0:
                        norm_ahead(ch(0, 2))
                    for u in range(8):
                        maxima(ch(0, 0), u)
                    max_parts(ch(0, 0))

                def step(prep, mxc, att_c, done, ahead):
                    fill(prep, done)
                    for n in range(10):
                        if n < 4 and mxc is not None:
                            maxima(mxc, 2 * n)
                            maxima(mxc, 2 * n + 1)
                        if n == 4:
                            if mxc is not None:
                                max_parts(mxc)
                            if layer == 0 and done is not None:
                                pool_tokens(done)
                        if n >= 3 and n % 2 == 1:
                            divide(att_c, (n - 3) // 2)
                        if n == 6 and layer == 0 and ahead is not None:
                            norm_ahead(ahead)
                    if prep is not None:
                        values(prep)

                def last(c):
                    fill(None, c)
                    if layer == 0:
                        pool_tokens(c)
                walk(dve, layer, first, step, last)

                if layer == 0:
                    dve.wait_ge(g_pe, 2)
                    nc.vector.tensor_copy(lg[:], s1[1][:, 0:E]).then_inc(g_dve, 1)
                    dve.wait_ge(g_dve, 1)
                    dve.wait_ge(c_set, 5)
                    other = lg[:].rearrange("b (o e) -> b o e", o=1).broadcast_to([128, E, E])
                    own = lg[:].rearrange("b (e o) -> b e o", o=1).broadcast_to([128, E, E])
                    nc.vector.tensor_tensor(beat[:], other, own, ALU.is_gt).then_inc(g_dve, 1)
                    nc.vector.tensor_tensor(tie[:], other, own, ALU.is_equal).then_inc(g_dve, 1)
                    nc.vector.tensor_reduce(nmax[:], lg[:], AX.X, ALU.max, negate=True).then_inc(g_dve, 1)
                    dve.wait_ge(g_dve, 4)
                    nc.vector.tensor_tensor(tie[:], tie[:], tri[:], ALU.mult).then_inc(g_dve, 1)
                    dve.wait_ge(g_dve, 5)
                    nc.vector.tensor_tensor(beat[:], beat[:], tie[:], ALU.add).then_inc(g_dve, 1)
                    dve.wait_ge(g_dve, 6)
                    nc.vector.tensor_reduce(rank[:], beat[:], AX.X, ALU.add).then_inc(g_dve, 1)
                    dve.wait_ge(g_dve, 7)
                    dve.wait_ge(g_act, 2)
                    nc.vector.scalar_tensor_tensor(out=ex[:], in0=rank[:], scalar=1.5, in1=ex[:],
                                                   op0=ALU.is_lt, op1=ALU.mult).then_inc(g_dve, 1)
                    dve.wait_ge(g_dve, 8)
                    nc.vector.tensor_reduce(gsum[:], ex[:], AX.X, ALU.add).then_inc(g_dve, 1)
                    dve.wait_ge(g_dve, 9)
                    nc.vector.reciprocal(rsum[:], gsum[:]).then_inc(g_dve, 1)
                    dve.wait_ge(g_dve, 10)
                    nc.vector.tensor_scalar(gexp[:], ex[:].rearrange("b (e o) -> b e o", o=1).broadcast_to([128, E, R]),
                                            rsum[:], None, ALU.mult).then_inc(g_dve, 1)
                    dve.wait_ge(g_pe, 3)
                    for j, p in enumerate("qkvo"):
                        nc.vector.tensor_scalar(sg[p][:], s1[0][:, 0:B], s_col[:, j:j + 1], None, ALU.mult).then_inc(g_dve, 1)
                    dve.wait_ge(g_dve, 15)

        @block.tensor
        def _(pe):
            pe.wait_ge(d_w, 16 * (NW + 12))
            pe.wait_ge(c_set, 5)
            for n in range(NW):
                if n >= 2:
                    pe.wait_ge(w_done, n - 1)
                nc.tensor.transpose(pa[n % 2][:, 0:128], w_nat[:, n, :], ident[:]).then_inc(w_ps, 1)
            pe.wait_ge(w_done, NW - 1)
            nc.tensor.transpose(pa[NW % 2][:, 0:GH], gw1_nat[:], ident[0:GH, 0:GH]).then_inc(w_ps, 1)
            pe.wait_ge(w_done, NW + 2)
            pe.wait_ge(c_zero, 13)
            pe.wait_ge(d_ones, 64)

            def W(name):
                return wT[:, WI[name], :]

            def fill(c, done):
                if c is not None and c.layer == 0:
                    pe.wait_ge(ln_x, c.c * NP + NP)
                    if after(c.n):
                        pe.wait_ge(v_ok, c.n)
                    for p in range(NP):
                        last = nc.tensor.transpose(pa[0][:, 128 * p:128 * p + 128], xn[c.k][:, p, :], ident[:])
                    last.then_inc(xT_ps, 1)
                    pe.wait_ge(d_ctx[c.k], c.u * 16 + 16)
                    if after(c.n):
                        pe.wait_ge(k_r, c.n)
                    if after(c.c - 3):
                        pe.wait_ge(zT_ok, c.c - 3)
                    for p in range(NP):
                        last = nc.tensor.transpose(pa[1][:, 128 * p:128 * p + 128], ctx_sb[c.k][:, p, :], ident[:])
                    last.then_inc(cT_ps, 1)
                    pe.wait_ge(xT_ok, c.c + 1)
                    nc.tensor.matmul(pa[0][:], W("wq"), fT[:], start=True, stop=True).then_inc(q_ps, 1)
                    pe.wait_ge(cT_ok, c.c + 1)
                    nc.tensor.matmul(pa[1][:], W("wk"), cT[:], start=True, stop=True).then_inc(k_ps, 1)
                if done is not None and done.layer == 0:
                    pe.wait_ge(l2_z, done.c * NP + NP)
                    if c is not None:
                        pe.wait_ge(k_r, c.n + 1)
                    else:
                        pe.wait_ge(k_r, NC)
                        if after(done.c):
                            pe.wait_ge(zT_ok, done.c)
                    for p in range(NP):
                        last = nc.tensor.transpose(pa[1][:, 128 * p:128 * p + 128], z[:, p, :], ident[:])
                    last.then_inc(zT_ps, 1)
                if done is not None and done.layer == 1:
                    pe.wait_ge(att_ok, done.n * NP + NP)
                    pe.wait_ge(v_ok, (c.n if c is not None else 2 * NC))
                    if c is None and after(done.c):
                        pe.wait_ge(o_ok, done.c)
                    for p in range(NP):
                        last = nc.tensor.transpose(pa[0][:, 128 * p:128 * p + 128], att[:, p, :], ident[:])
                    last.then_inc(aT_ps, 1)
                if c is not None and c.layer == 1:
                    pe.wait_ge(f_ok, c.c + 1)
                    pe.wait_ge(k_r, c.n)
                    nc.tensor.matmul(pa[1][:], W("qV"), cT[:], start=True, stop=True).then_inc(xv_ps["q"], 1)
                if done is not None and done.layer == 1:
                    pe.wait_ge(aT_ok, done.c + 1)
                    nc.tensor.matmul(pa[0][:], W("oV"), attT[:], start=True, stop=True).then_inc(xv_ps["o"], 1)
                if c is not None and c.layer == 1:
                    pe.wait_ge(xv_ok["q"], c.c + 1)
                    nc.tensor.matmul(pa[1][:], W("qW"), cT[:], start=True, stop=False)
                    nc.tensor.matmul(pa[1][:], W("qU"), xvs["q"][:], start=False, stop=True).then_inc(q_ps, 1)
                if done is not None and done.layer == 1:
                    pe.wait_ge(xv_ok["o"], done.c + 1)
                    for p in range(NP):
                        cols = slice(128 * p, 128 * p + 128)
                        nc.tensor.matmul(pa[0][:, cols], attT[:, cols], W("oW"), start=True, stop=False)
                        last = nc.tensor.matmul(pa[0][:, cols], xvs["o"][:, cols], W("oU"), start=False, stop=True)
                    last.then_inc(o_ps, 1)
                if c is not None and c.layer == 1:
                    pe.wait_ge(q_r, c.n + 1)
                    nc.tensor.matmul(pa[1][:], W("kV"), cT[:], start=True, stop=True).then_inc(xv_ps["k"], 1)
                    if done is not None:
                        pe.wait_ge(o_ok, done.c + 1)
                    else:
                        pe.wait_ge(v_ok, c.n)
                    nc.tensor.matmul(pa[0][:], W("vV"), cT[:], start=True, stop=True).then_inc(xv_ps["v"], 1)
                    pe.wait_ge(xv_ok["k"], c.c + 1)
                    nc.tensor.matmul(pa[1][:], W("kW"), cT[:], start=True, stop=False)
                    nc.tensor.matmul(pa[1][:], W("kU"), xvs["k"][:], start=False, stop=True).then_inc(k_ps, 1)

            def values(c):
                if c.layer == 0:
                    pe.wait_ge(q_r, c.n + 1)
                else:
                    pe.wait_ge(xv_ok["v"], c.c + 1)
                for p in range(NP):
                    cols = slice(128 * p, 128 * p + 128)
                    if c.layer == 0:
                        last = nc.tensor.matmul(pa[0][:, cols], cT[:, cols], W("wv"), start=True, stop=True)
                    else:
                        nc.tensor.matmul(pa[0][:, cols], cT[:, cols], W("vW"), start=True, stop=False)
                        last = nc.tensor.matmul(pa[0][:, cols], xvs["v"][:, cols], W("vU"), start=False, stop=True)
                last.then_inc(v_ps, 1)

            def scores(c, unit):
                p, g = unit // 2, unit % 2
                if unit == 0:
                    pe.wait_ge(d_qget[c.k], c.u * 96 + 96)
                    pe.wait_ge(d_kget[c.k], c.u * 96 + 96)
                    if after(c.n):
                        pe.wait_ge(mT_ok, c.n)
                if after(c.n * 8 + (unit - 1)):
                    pe.wait_ge(max_ok, c.n * 8 + (unit - 1))
                for j in range(4):
                    for a in range(2):
                        h = 2 * (4 * g + j) + a
                        last = nc.tensor.matmul(s1[unit % 2][S * a:S * a + S, 128 * j:128 * j + 128],
                                                qst[c.k][0:ROWS, h, p, :], kbd[c.k][0:ROWS, h, :, p], start=True, stop=True)
                last.then_inc(sc_ps, 1)

            def maxT(c):
                pe.wait_ge(m_parts, c.n + 1)
                for b in range(2):
                    last = nc.tensor.transpose(mT_ps[0:96, b, :], mxp[:, b].rearrange("q s g p -> q (s g p)"), identb[:])
                last.then_inc(mT_pe, 1)

            def shifted(c, n):
                p, half = n // 2, n % 2
                if n == 0:
                    pe.wait_ge(d_mget[c.k], c.u * 16 + 16)
                if after(c.n * 8 + (n - 1)):
                    pe.wait_ge(exp_ok, c.n * 8 + (n - 1))
                for j in range(8):
                    h = 8 * half + j
                    last = nc.tensor.matmul(s2[n % 2][:, S * j:S * j + S], kbd[c.k][:, h, :, p], qst[c.k][:, h, p, :],
                                            start=True, stop=True)
                last.then_inc(s2_ps, 1)

            def times_values(c, n):
                p, half = n // 2, n % 2
                pe.wait_ge(exp_ok, c.n * 8 + (n + 1))
                if n == 0:
                    pe.wait_ge(v_ok, c.n + 1)
                if half == 0 and after(c.n * NP + (p - 1)):
                    pe.wait_ge(att_ok, c.n * NP + (p - 1))
                for j in range(8):
                    h = 8 * half + j
                    g = h // 4
                    last = nc.tensor.matmul(av[p % 2][32 * (h % 4):32 * (h % 4) + 2 * VW, S * g:S * g + S],
                                            vbd[c.k][:, p, h, :], prob[n % 4][:, j, :], start=True, stop=True)
                last.then_inc(av_ps, 1)

            def turn(c, p):
                pe.wait_ge(av_ok, c.n * NP + (p + 1))
                for s in range(2):
                    last = nc.tensor.transpose(av[p % 2][:, 256 + 128 * s:384 + 128 * s],
                                               av_sb[p % 2][:, 128 * s:128 * s + 128], ident[:])
                last.then_inc(avT_ps, 1)

            for layer in range(2):
                def first(ch):
                    for j in range(2):
                        fill(ch(0, j), None)
                        values(ch(0, j))
                    for u in range(8):
                        scores(ch(0, 0), u)
                    maxT(ch(0, 0))

                def step(prep, mxc, att_c, done, ahead):
                    fill(prep, done)
                    for n in range(10):
                        if n < 8:
                            shifted(att_c, n)
                        if n < 4 and mxc is not None:
                            scores(mxc, 2 * n)
                            scores(mxc, 2 * n + 1)
                        if 1 <= n <= 8:
                            times_values(att_c, n - 1)
                        if n == 5 and mxc is not None:
                            maxT(mxc)
                        if n == 9 and prep is not None:
                            values(prep)
                        if n >= 3 and n % 2 == 1:
                            turn(att_c, (n - 3) // 2)

                walk(pe, layer, first, step, lambda c: fill(None, c))
                if layer == 0:
                    pe.wait_ge(pool_ok, NC)
                    pe.wait_ge(mT_ok, NC)
                    pe.wait_ge(max_ok, 8 * NC)
                    nc.tensor.matmul(s1[0][0:GH, 0:B], gw1T[:], pooled[:], start=True, stop=True).then_inc(g_pe, 1)
                    pe.wait_ge(g_act, 1)
                    nc.tensor.matmul(s1[1][:, 0:E], hid[:], gw2T[:], start=True, stop=True).then_inc(g_pe, 1)
                    pe.wait_ge(g_dve, 11)
                    nc.tensor.transpose(s1[0][:, 0:B], gexp[:].rearrange("b e r -> b (e r)"), ident[:]).then_inc(g_pe, 1)
                    pe.wait_ge(g_dve, 15)


_P = ("Wm", "U", "S", "V", "b")
_INS = (["x", "ctx_1024", "L0_xattn_Wq", "L0_xattn_Wk", "L0_xattn_Wv",
         "L0_ffn_gw1", "L0_ffn_gb1", "L0_ffn_gw2", "L0_ffn_gb2"]
        + ["L0_ffn_" + p + s for p in "qkvo" for s in _P])
_OUTS = [((B, S, D), 'float32')]


def kernel(**inputs):
    import numpy as _np
    import concourse.bacc as _bacc
    from concourse import mybir as _mybir
    from concourse.bass_utils import run_bass_kernel_spmd as _run

    nc = _bacc.Bacc("TRN2", target_bir_lowering=False, num_devices=1)
    arrays, args = {}, []
    for name in _INS:
        a = _np.ascontiguousarray(inputs[name])
        arrays[f"in_{name}_dram"] = a
        args.append(nc.dram_tensor(f"in_{name}_dram", a.shape, _mybir.dt.from_np(a.dtype), kind="ExternalInput").ap())
    for i, (shape, dtype) in enumerate(_OUTS):
        dt = _mybir.dt.from_np(_np.dtype(dtype))
        args.append(nc.dram_tensor(f"out_{i}_dram", shape, dt, kind="ExternalOutput").ap())
    xattn_ffn_kernel(nc, *args)
    r = _run(nc, [arrays], core_ids=[0])
    got = tuple(r.results[0][f"out_{i}_dram"] for i in range(len(_OUTS)))
    return got[0]
```

```python
import concourse.bass as bass
from concourse import mybir
from contextlib import ExitStack


B, S, D = 128, 64, 128
H, DH = 16, 8
E, R, GH = 8, 16, 32
NP = 4
TOK = NP * 2 * S
NC = B // (2 * NP)
EPS = 1e-5
SCALE = DH ** -0.5
PARTS = 3
SLOTS = 6
ROWS = 2 * SLOTS * DH
UNIT_H = H // 2
VW = DH + 1


class Chunk:

    def __init__(self, layer, it, off):
        self.layer = layer
        self.c = it * 2 + off
        self.n = it * 2 + (off + NC * layer)
        self.k = off % 2
        self.u = it + (off // 2 + NC // 2 * layer)


def after(value):
    return not isinstance(value, int) or value > 0


def xattn_ffn_kernel(nc, x, ctx_in, wq, wk, wv, gw1, gb1, gw2, gb2,
                     qWm, qU, qS, qV, qb, kWm, kU, kS, kV, kb,
                     vWm, vU, vS, vV, vb, oWm, oU, oS, oV, ob, out):
    f32, bf16 = mybir.dt.float32, mybir.dt.bfloat16
    ALU, ACT, AX = mybir.AluOpType, mybir.ActivationFunctionType, mybir.AxisListType

    x_d = x.rearrange("(p b) t f -> (b t) p f", b=2)
    c_d = ctx_in.rearrange("(p b) t f -> (b t) p f", b=2)
    o_d = out.rearrange("(p b) t f -> (b t) p f", b=2)

    qpd = [nc.dram_tensor(f"q_parts_dram{k}", [H, DH, SLOTS, TOK], bf16, kind="Internal").ap() for k in range(2)]
    kpd = [nc.dram_tensor(f"k_parts_dram{k}", [H, DH, SLOTS, TOK], bf16, kind="Internal").ap() for k in range(2)]

    NAMES = ["wq", "wk", "wv", "qW", "kW", "vW", "oW", "qV", "kV", "vV", "oV", "qU", "kU", "vU", "oU"]
    NW = len(NAMES)
    SCALED = ("wq", "qW", "qU")
    WI = {n: i for i, n in enumerate(NAMES)}
    w_src = dict(wq=wq, wk=wk, wv=wv, qW=qWm, kW=kWm, vW=vWm, oW=oWm)
    for n, v in (("qV", qV), ("kV", kV), ("vV", vV), ("oV", oV)):
        w_src[n] = v.rearrange("e r d -> (e r) d")
    u_src = dict(qU=qU, kU=kU, vU=vU, oU=oU)

    with ExitStack() as st:
        def sb(name, shape, dt=f32):
            return st.enter_context(nc.sbuf_tensor(name, shape, dt))

        def sem(name):
            return st.enter_context(nc.semaphore(name))

        def sem2(name):
            return [sem(f"{name}{k}") for k in range(2)]

        x1 = sb("x1", [128, NC * NP, D])
        zT = sb("zT", [128, NC * TOK])
        kbd = [sb(f"kbd{k}", [ROWS, H, 2 * S, NP], bf16) for k in range(2)]
        qst = [sb(f"qst{k}", [ROWS, H, NP, S], bf16) for k in range(2)]
        w_nat = zT[:, 0:NW * D].rearrange("p (n f) -> p n f", n=NW)
        prob = [sb(f"prob{j}", [128, 8, S]) for j in range(4)]
        vbd = [sb(f"vbd{k}", [128, NP, H, 2 * VW]) for k in range(2)]
        wT = sb("wT", [128, NW, D])
        ident = sb("ident", [128, 128])
        identb = sb("identb", [128, 128], bf16)
        ctx_sb = [sb(f"ctx_sb{k}", [128, NP, D]) for k in range(2)]
        xn = [sb(f"xn{k}", [128, NP, D]) for k in range(2)]
        z = sb("z", [128, NP, D])
        fT = sb("fT", [128, TOK])
        cT = sb("cT", [128, TOK])
        qpart = [sb(f"qpart{k}", [128, PARTS, TOK], bf16) for k in range(2)]
        kpart = [sb(f"kpart{k}", [128, PARTS, TOK], bf16) for k in range(2)]
        q_rest = sb("q_rest", [128, TOK])
        k_rest = sb("k_rest", [128, TOK])
        GP = UNIT_H // 2 * NP
        mx = sb("mx", [128, 4, GP])
        mxp = sb("mxp", [128, 4, PARTS, GP], bf16)
        mx_rest = sb("mx_rest", [128, 4, GP])
        mxT = [sb(f"mxT{k}", [2 * PARTS * GP, 2, 128], bf16) for k in range(2)]
        pick_of = sb("pick_of", [2 * PARTS * GP, 2, GP])
        pick = sb("pick", [2 * PARTS * GP, GP, 2 * S], bf16)
        av_sb = [sb(f"av_sb{j}", [128, 256]) for j in range(2)]
        rden = sb("rden", [128, 2, 8, 2])
        att = [sb(f"att{k}", [128, NP, D]) for k in range(2)]
        stats = sb("stats", [128, NP, 6])
        mv = sb("mv", [128, NP, 2])
        rstd = sb("rstd", [128, NP])
        m_half = sb("m_half", [128, NP])
        eps_c = sb("eps_c", [128, NP])
        stats2 = sb("stats2", [128, NP, 6])
        mv2 = sb("mv2", [128, NP, 2])
        rstd2 = sb("rstd2", [128, NP])
        shift = sb("shift", [128, NP])
        shift2 = sb("shift2", [128, NP])
        m_one = sb("m_one", [128, NP])
        xvs = {p: sb("xvs_" + p, [128, TOK]) for p in "vo"}
        for k, p in enumerate("qk"):
            xvs[p] = xn[k][:].rearrange("e p f -> e (p f)")
        attT, xo, osb = fT, z, ctx_sb
        vb_bc = sb("vb_bc", [128, D])
        ob_bc = sb("ob_bc", [128, D])
        qb_c = sb("qb_c", [128, 1])
        qbs_c = sb("qbs_c", [128, 1])
        kb_c = sb("kb_c", [128, 1])
        s_col = sb("s_col", [128, 4])
        gw1_nat = sb("gw1_nat", [GH, D])
        gw1T = sb("gw1T", [128, GH])
        gb1_c = sb("gb1_c", [GH, 1])
        gw2T = sb("gw2T", [GH + 1, E])
        hid = sb("hid", [GH + 1, B])
        pooled = sb("pooled", [128, B])
        lg = sb("lg", [128, E])
        tri = sb("tri", [128, E, E])
        beat = sb("beat", [128, E, E])
        tie = sb("tie", [128, E, E])
        rank = sb("rank", [128, E])
        nmax = sb("nmax", [128, 1])
        ex = sb("ex", [128, E])
        gsum = sb("gsum", [128, 1])
        rsum = sb("rsum", [128, 1])
        gexp = sb("gexp", [128, E, R])
        sg = {p: sb("sg_" + p, [128, B]) for p in "qkvo"}

        def pb(name):
            return st.enter_context(nc.psum_tensor(name, [128, 512], f32))
        s1 = [pb(f"ps_s1_{j}") for j in range(2)]
        s2 = [pb(f"ps_s2_{j}") for j in range(2)]
        av = [pb(f"ps_av_{j}") for j in range(2)]
        pa = [pb(f"ps_a_{j}") for j in range(2)]
        mT_ps = s1[0][:, 0:128].bitcast(bf16).rearrange("p (b c) -> p b c", b=2)

        d_w3, d_w, d_vec = sem("d_w3"), sem("d_w"), sem("d_vec")
        d_x, d_ctx = sem2("d_x"), sem2("d_ctx")
        d_qput, d_kput = sem2("d_qput"), sem2("d_kput")
        d_qget, d_kget = sem2("d_qget"), sem2("d_kget")
        d_out = sem2("d_out")
        c_set = sem("c_set")
        c_tri = sem("c_tri")
        c_vbd, c_kbd, c_av = sem("c_vbd"), sem("c_kbd"), sem("c_av")
        c_pick = sem("c_pick")
        w_ps, w_done = sem("w_ps"), sem("w_done")
        ln_mv, ln_rs, ln_x = sem("ln_mv"), sem("ln_rs"), sem("ln_x")
        l2_mv, l2_rs, l2_z = sem("l2_mv"), sem("l2_rs"), sem("l2_z")
        xT_ps, xT_ok, cT_ps, cT_ok = sem("xT_ps"), sem("xT_ok"), sem("cT_ps"), sem("cT_ok")
        ln_ve, l2_ve = sem("ln_ve"), sem("l2_ve")
        zT_ps, zT_ok, pool_ok = sem("zT_ps"), sem("zT_ok"), sem("pool_ok")
        q_ps, q_hi, q_r, q_mid, q_lo = sem("q_ps"), sem("q_hi"), sem("q_r"), sem("q_mid"), sem("q_lo")
        k_ps, k_hi, k_r, k_mid, k_lo = sem("k_ps"), sem("k_hi"), sem("k_r"), sem("k_mid"), sem("k_lo")
        v_ps, v_ok = sem("v_ps"), sem("v_ok")
        sc_ps, max_ok = sem("sc_ps"), sem("max_ok")
        m_hi, m_r, m_mid, m_parts = sem("m_hi"), sem("m_r"), sem("m_mid"), sem("m_parts")
        mT_pe, mT_ok = sem("mT_pe"), sem("mT_ok")
        s2_ps, exp_ok, av_ps, av_ok, avT_ps = sem("s2_ps"), sem("exp_ok"), sem("av_ps"), sem("av_ok"), sem("avT_ps")
        rden_ok, att_ok, add_ok = sem("rden_ok"), sem("att_ok"), sem("add_ok")
        xv_ps = {p: sem("xv_ps_" + p) for p in "qkvo"}
        xv_ok = {p: sem("xv_ok_" + p) for p in "qkvo"}
        f_ok = sem("f_ok")
        aT_ps, aT_ok, o_ps, o_ok, xo_ok = sem("aT_ps"), sem("aT_ok"), sem("o_ps"), sem("o_ok"), sem("xo_ok")
        g_pe, g_act, g_dve = sem("g_pe"), sem("g_act"), sem("g_dve")

        block = st.enter_context(nc.Block())

        UNITS = ({1: (0, 1), 2: (2, 3), 3: (4, 5), 4: (6, 7)}, {3: (0, 1), 4: (2, 3), 5: (4, 5), 6: (6, 7)})
        LAST_UNITS = (4, 6)
        MAX_T = (7, 7)

        def walk(eng, layer, first, step, last):
            ch = lambda it, off: Chunk(layer, it, off)
            first(ch)
            for i in range(2):
                step(ch(0, i + 2), ch(0, i + 1), ch(0, i), ch(0, i - 1) if i else None, ch(0, i + 3))
            looped = NC - 4
            with eng.Fori(1, looped // 2) as it:
                for k in range(2):
                    step(ch(it, k + 2), ch(it, k + 1), ch(it, k), ch(it, k - 1), ch(it, k + 3))
            for i in range(looped, NC):
                prep, mxc, ahead = (ch(0, i + j) if i + j < NC else None for j in (2, 1, 3))
                step(prep, mxc, ch(0, i), ch(0, i - 1), ahead)
            last(ch(0, NC - 1))

        @block.sync
        def _(sp):
            def weight(n, arrived):
                name = NAMES[n]
                if name in w_src:
                    sp.dma_start(w_nat[:, n, :], w_src[name]).then_inc(arrived, 16)
                else:
                    sp.dma_start(w_nat[:, n, :].rearrange("o (e r) -> o e r", e=E),
                                 u_src[name].rearrange("e o r -> o e r")).then_inc(arrived, 16)

            def vectors():
                sp.dma_start(gw1_nat[:], gw1).then_inc(d_vec, 16)
                sp.dma_start(vb_bc[:], vb[None, :].broadcast_to([128, D])).then_inc(d_vec, 16)
                sp.dma_start(ob_bc[:], ob[None, :].broadcast_to([128, D])).then_inc(d_vec, 16)
                sp.dma_start(qb_c[:], qb[:, None]).then_inc(d_vec, 16)
                sp.dma_start(kb_c[:], kb[:, None]).then_inc(d_vec, 16)
                for j, s_ in enumerate((qS, kS, vS, oS)):
                    sp.dma_start(s_col[:, j:j + 1], s_.rearrange("e r -> (e r)")[:, None]).then_inc(d_vec, 16)
                sp.dma_start(gb1_c[:], gb1[:, None]).then_inc(d_vec, 16)
                sp.dma_start(gw2T[0:GH, :], gw2.rearrange("e g -> g e"), allow_slow_non_contiguous=True).then_inc(d_vec, 16)
                sp.dma_start(gw2T[GH:GH + 1, :], gb2[None, :]).then_inc(d_vec, 16)

            def held(*values):
                return [v if isinstance(v, int) else sp.snap(sp.to_reg(v)) for v in values]

            def load(c):
                came, turned = held(c.u * 16, c.n - 1)
                if after(came):
                    sp.wait_ge(d_x[c.k], came)
                sp.dma_start(x1[:, bass.ds(c.c * NP, NP), :], x_d[:, bass.ds(c.c * NP, NP), :]).then_inc(d_x[c.k], 16)
                if after(turned):
                    sp.wait_ge(cT_ps, turned)
                sp.dma_start(ctx_sb[c.k][:], c_d[:, bass.ds(c.c * NP, NP), :]).then_inc(d_ctx[c.k], 16)

            def put_q(c):
                cut, read = held(c.n + 1, c.u * 16)
                sp.wait_ge(q_lo, cut)
                if after(read):
                    sp.wait_ge(d_qget[c.k], read)
                slots = qpd[c.k].rearrange("h d s t -> (h d) s t")
                sp.dma_start(slots[:, 0:4, :].rearrange("f (r s) t -> f r (s t)", r=2),
                             qpart[c.k][:, 0:2, :].rearrange("f s (r t) -> f r (s t)", r=1).broadcast_to([128, 2, 2 * TOK])
                             ).then_inc(d_qput[c.k], 16)
                sp.dma_start(slots[:, 4:6, :], qpart[c.k][:, 0:3:2, :]).then_inc(d_qput[c.k], 16)

            def put_k(c):
                cut, read = held(c.n + 1, c.u * 32)
                sp.wait_ge(k_lo, cut)
                if after(read):
                    sp.wait_ge(d_kget[c.k], read)
                slots = kpd[c.k].rearrange("h d s t -> (h d) s t")
                sp.dma_start(slots[:, 0:6:2, :], kpart[c.k][:]).then_inc(d_kput[c.k], 16)
                sp.dma_start(slots[:, 1:5:2, :], kpart[c.k][:, 1:3, :]).then_inc(d_kput[c.k], 16)
                sp.dma_start(slots[:, 5, :], kpart[c.k][:, 2, :]).then_inc(d_kput[c.k], 16)

            def put(c):
                if c.layer == 0:
                    put_k(c)
                    put_q(c)
                else:
                    put_q(c)
                    put_k(c)

            def get(c):
                freed, q_stored, k_stored = held((c.n - 1) * 8, c.u * 32 + 32, c.u * 48 + 48)
                if after(freed):
                    sp.wait_ge(s2_ps, freed)

                def get_q():
                    sp.wait_ge(d_qput[c.k], q_stored)
                    sp.dma_start(qst[c.k][:].rearrange("r h p t -> r h (p t)"),
                                 qpd[c.k].rearrange("h d s (b t) -> (d s b) h t", b=2)).then_inc(d_qget[c.k], 16)

                def get_k():
                    sp.wait_ge(d_kput[c.k], k_stored)
                    for b in range(2):
                        sp.dma_start(kbd[c.k][b:ROWS:2, :, S * b:S * b + S, :].rearrange("r h t p -> r h (t p)"),
                                     kpd[c.k].rearrange("h d s (b t) -> b (d s) h t", b=2)[b]).then_inc(d_kget[c.k], 16)
                if c.layer == 0:
                    get_k()
                    get_q()
                else:
                    get_q()
                    get_k()

            for layer in range(2):
                def first(ch):
                    if layer == 0:
                        load(ch(0, 0))
                        for n in range(3):
                            weight(n, d_w3)
                        load(ch(0, 1))
                        for n in range(3, NW):
                            weight(n, d_w)
                        put(ch(0, 0))
                        vectors()
                        load(ch(0, 2))
                    else:
                        put(ch(0, 0))
                    for j in range(2):
                        if j == 1:
                            put(ch(0, 1))
                        if layer == 0:
                            sp.wait_ge(c_kbd, j + 1)
                        get(ch(0, j))

                def step(prep, mxc, att_c, done, ahead):
                    if layer == 0 and ahead is not None:
                        load(ahead)
                    if prep is not None:
                        put(prep)
                    if prep is not None:
                        get(prep)
                    if layer == 1 and done is not None:
                        store(done)

                def store(c):
                    ready, at = held(c.c + 1, c.c * NP)
                    sp.wait_ge(o_ok, ready)
                    sp.dma_start(o_d[:, bass.ds(at, NP), :], osb[c.k][:]).then_inc(d_out[c.k], 16)
                walk(sp, layer, first, step, store if layer == 1 else (lambda c: None))
            for k in range(2):
                sp.wait_ge(d_out[k], 16 * NC // 2)

        @block.gpsimd
        def _(pool):
            nc.gpsimd.memset(ident[:], 0.0).then_inc(c_set, 1)
            nc.gpsimd.memset(m_half[:], -0.5).then_inc(c_set, 1)
            nc.gpsimd.memset(eps_c[:], EPS).then_inc(c_set, 1)
            nc.gpsimd.memset(m_one[:], -1.0).then_inc(c_set, 1)
            pool.wait_ge(c_set, 4)
            nc.gpsimd.affine_select(out=ident[:], in_=ident[:], compare_op=ALU.not_equal, fill=1.0, base=0,
                                    pattern=[[-1, 128]], channel_multiplier=1).then_inc(c_set, 1)
            pool.wait_ge(c_set, 5)

            def constants():
                nc.gpsimd.tensor_copy(identb[:], ident[:]).then_inc(c_tri, 1)
                nc.gpsimd.memset(tri[:], 1.0).then_inc(c_tri, 1)
                pool.wait_ge(c_tri, 2)
                nc.gpsimd.affine_select(out=tri[:], in_=tri[:], compare_op=ALU.is_ge, fill=0.0, base=-1,
                                        pattern=[[1, E], [-1, E]], channel_multiplier=0).then_inc(c_tri, 1)
                pool.wait_ge(c_tri, 3)

            def value_buffers():
                for k in range(2):
                    nc.gpsimd.memset(vbd[k][:], 0.0).then_inc(c_vbd, 1)
                pool.wait_ge(c_vbd, 2)
                for k in range(2):
                    for b in range(2):
                        nc.gpsimd.memset(vbd[k][S * b:S * b + S, :, :, VW * b + DH:VW * b + VW], 1.0).then_inc(c_vbd, 1)
                        pool.wait_ge(c_vbd, 2 * k + b + 3)

            def low_part(c, which):
                mid, rest, part, order, lo = {"q": (q_mid, q_rest, qpart, (1, 2), q_lo),
                                              "k": (k_mid, k_rest, kpart, (1, 0), k_lo)}[which]
                pool.wait_ge(mid, c.n + 1)
                nc.gpsimd.tensor_tensor(part[c.k][:, order[1], :], rest[:], part[c.k][:, order[0], :],
                                        ALU.subtract).then_inc(lo, 1)

            def low_parts(c):
                for which in ("kq", "qk")[c.layer]:
                    low_part(c, which)

            def ahead_rstd(c):
                pool.wait_ge(ln_mv, c.c * NP + NP)
                if after(c.c * NP):
                    pool.wait_ge(ln_x, c.c * NP)
                nc.gpsimd.tensor_tensor(rstd[:], mv[:, :, 1], eps_c[:], ALU.add).then_inc(ln_ve, 1)
                pool.wait_ge(ln_ve, c.c * 3 + 1)
                nc.gpsimd.tensor_tensor(rstd[:], rstd[:], m_half[:], ALU.pow).then_inc(ln_ve, 1)
                pool.wait_ge(ln_ve, c.c * 3 + 2)
                nc.gpsimd.tensor_tensor(shift[:], mv[:, :, 0], rstd[:], ALU.mult).then_inc(ln_ve, 1)
                pool.wait_ge(ln_ve, c.c * 3 + 3)
                nc.gpsimd.tensor_tensor(shift[:], shift[:], m_one[:], ALU.mult).then_inc(ln_rs, 1)

            def result_rstd(c):
                pool.wait_ge(l2_mv, c.c * NP + NP)
                if after(c.c * NP):
                    pool.wait_ge(l2_z, c.c * NP)
                nc.gpsimd.tensor_tensor(rstd2[:], mv2[:, :, 1], eps_c[:], ALU.add).then_inc(l2_ve, 1)
                pool.wait_ge(l2_ve, c.c * 3 + 1)
                nc.gpsimd.tensor_tensor(rstd2[:], rstd2[:], m_half[:], ALU.pow).then_inc(l2_ve, 1)
                pool.wait_ge(l2_ve, c.c * 3 + 2)
                nc.gpsimd.tensor_tensor(shift2[:], mv2[:, :, 0], rstd2[:], ALU.mult).then_inc(l2_ve, 1)
                pool.wait_ge(l2_ve, c.c * 3 + 3)
                nc.gpsimd.tensor_tensor(shift2[:], shift2[:], m_one[:], ALU.mult).then_inc(l2_rs, 1)

            def residual(c, pairs):
                for p in pairs:
                    pool.wait_ge(att_ok, c.n * NP + (p + 1))
                    xp = x1[:, bass.ds(c.c * NP + p, 1), :]
                    nc.gpsimd.tensor_tensor(xp, xp, att[c.k][:, p:p + 1, :], ALU.add).then_inc(add_ok, 1)

            def fetch(c):
                if after(c.c):
                    pool.wait_ge(v_ps, c.n)
                pool.wait_ge(zT_ok, NC)
                nc.gpsimd.tensor_copy(cT[:], zT[:, bass.ds(c.c * TOK, TOK)]).then_inc(f_ok, 1)

            for layer in range(2):
                def first(ch):
                    if layer == 0:
                        ahead_rstd(ch(0, 0))
                        constants()
                        value_buffers()
                        ahead_rstd(ch(0, 1))
                    for j in range(2):
                        if layer == 1:
                            fetch(ch(0, j))
                        low_parts(ch(0, j))
                    if layer == 0:
                        ahead_rstd(ch(0, 2))
                    else:
                        fetch(ch(0, 2))

                def step(prep, mxc, att_c, done, ahead):
                    if layer == 0 and done is not None:
                        result_rstd(done)
                    if prep is not None:
                        low_parts(prep)
                    if layer == 1 and done is not None:
                        if after(done.c):
                            pool.wait_ge(o_ok, done.c)
                        nc.gpsimd.tensor_tensor(xo[:], x1[:, bass.ds(done.c * NP, NP), :],
                                                ob_bc[:, None, :].broadcast_to([128, NP, D]), ALU.add).then_inc(xo_ok, 1)
                    if layer == 0:
                        if ahead is not None:
                            ahead_rstd(ahead)
                        if att_c is not None:
                            residual(att_c, (0, 1, 2))
                    elif ahead is not None:
                        fetch(ahead)
                    if layer == 0 and att_c is not None:
                        residual(att_c, (3,))
                walk(pool, layer, first, step, lambda c: step(None, None, None, c, None))

        @block.scalar
        def _(act):
            def weights(names):
                for n in names:
                    act.wait_ge(w_ps, n + 1)
                    nc.scalar.activation(wT[:, n, :], pa[n % 2][:, 0:128], ACT.Copy,
                                         scale=SCALE if NAMES[n] in SCALED else 1.0).then_inc(w_done, 1)

            def ctx_turned(c):
                act.wait_ge(cT_ps, c.n + 1)
                nc.scalar.copy(cT[:], pa[1][:]).then_inc(cT_ok, 1)

            def x_turned(c):
                act.wait_ge(xT_ps, c.n + 1)
                nc.scalar.copy(fT[:], pa[0][:]).then_inc(xT_ok, 1)

            def att_turned(c):
                act.wait_ge(aT_ps, c.c + 1)
                nc.scalar.copy(attT[:], pa[1][:]).then_inc(aT_ok, 1)

            def z_turned(c):
                act.wait_ge(zT_ps, c.c + 1)
                nc.scalar.copy(zT[:, bass.ds(c.c * TOK, TOK)], pa[1][:]).then_inc(zT_ok, 1)

            def first_part(c, which):
                func = ACT.Relu if c.layer == 0 else ACT.Identity
                ps, put, stores, part, at, view, bias, bank, hi = {
                    "q": (q_ps, d_qput, 32, qpart, 0, "f (b p t) -> f p b t", qbs_c, pa[c.layer], q_hi),
                    "k": (k_ps, d_kput, 48, kpart, 2, "f (b t p) -> f p b t", kb_c, pa[1 - c.layer], k_hi)}[which]
                act.wait_ge(ps, c.n + 1)
                if after(c.u * stores):
                    act.wait_ge(put[c.k], c.u * stores)
                nc.scalar.activation(part[c.k][:, at, :].rearrange(view, b=2, p=NP),
                                     bank[:].rearrange("f (p b t) -> f p b t", p=NP, b=2), func,
                                     bias=bias[:] if c.layer else 0.0).then_inc(hi, 1)

            def second_part(c, which):
                rs, rest, part, mid = {"q": (q_r, q_rest, qpart, q_mid), "k": (k_r, k_rest, kpart, k_mid)}[which]
                act.wait_ge(rs, c.n + 1)
                nc.scalar.copy(part[c.k][:, 1, :], rest[:]).then_inc(mid, 1)

            def ahead_apply(c):
                act.wait_ge(ln_rs, c.c + 1)
                if after(c.c - 1):
                    act.wait_ge(xT_ps, c.c - 1)
                for p in range(NP):
                    nc.scalar.activation(xn[c.k][:, p:p + 1, :], x1[:, bass.ds(c.c * NP + p, 1), :], ACT.Identity,
                                         scale=rstd[:, p:p + 1], bias=shift[:, p:p + 1]).then_inc(ln_x, 1)

            def result_apply(c):
                act.wait_ge(l2_rs, c.c + 1)
                if after(c.c):
                    act.wait_ge(zT_ps, c.c)
                for p in range(NP):
                    nc.scalar.activation(z[:, p:p + 1, :], x1[:, bass.ds(c.c * NP + p, 1), :], ACT.Identity,
                                         scale=rstd2[:, p:p + 1], bias=shift2[:, p:p + 1]).then_inc(l2_z, 1)

            def values(c):
                if c.layer == 0:
                    act.wait_ge(v_ps, c.n + 1)
                    if after((c.n - 1) * 8):
                        act.wait_ge(av_ps, (c.n - 1) * 8)
                    for b in range(2):
                        last = nc.scalar.activation(
                            vbd[c.k][S * b:S * b + S, :, :, VW * b:VW * b + DH].rearrange("t p h d -> t (p h) d"),
                            pa[0][S * b:S * b + S, :].rearrange("t (p d) -> t p d", d=DH), ACT.Relu)
                    last.then_inc(v_ok, 1)

            def maxT(c):
                act.wait_ge(mT_pe, c.n + 1)
                if after((c.n - 1) * 8):
                    act.wait_ge(s2_ps, (c.n - 1) * 8)
                nc.scalar.copy(mxT[c.k][:], mT_ps[0:96]).then_inc(mT_ok, 1)

            for layer in range(2):
                def first(ch):
                    if layer == 0:
                        ahead_apply(ch(0, 0))
                        weights(range(3))
                    for j in range(2):
                        c = ch(0, j)
                        if layer == 0:
                            ctx_turned(c)
                            x_turned(c)
                            first_part(c, "k")
                            first_part(c, "q")
                            second_part(c, "k")
                            second_part(c, "q")
                            if j == 0:
                                ahead_apply(ch(0, 1))
                                act.wait_ge(c_vbd, 6)
                        else:
                            first_part(c, "q")
                            first_part(c, "k")
                            second_part(c, "q")
                            second_part(c, "k")
                        values(c)
                    if layer == 0:
                        ahead_apply(ch(0, 2))
                        weights(range(3, NW))
                        act.wait_ge(w_ps, NW + 1)
                        nc.scalar.activation(gw1T[:], pa[NW % 2][:, 0:GH], ACT.Copy, scale=1.0 / S).then_inc(w_done, 1)
                        act.wait_ge(d_vec, 12 * 16)
                        nc.scalar.mul(qbs_c[:], qb_c[:], SCALE).then_inc(w_done, 1)
                    maxT(ch(0, 0))

                def step(prep, mxc, att_c, done, ahead):
                    g = att_c.n * 8
                    if layer == 0 and prep is not None:
                        ctx_turned(prep)
                    for n in range(9):
                        if n < 8:
                            act.wait_ge(s2_ps, g + (n + 1))
                            if after(g + (n - 3)):
                                act.wait_ge(av_ps, g + (n - 3))
                            nc.scalar.activation(prob[n % 4][:].rearrange("p h t -> p (h t)"), s2[n % 2][:],
                                                 ACT.Exp).then_inc(exp_ok, 1)
                        if prep is not None:
                            if n == 1:
                                if layer == 0:
                                    x_turned(prep)
                                first_part(prep, "kq"[layer])
                            if n == 2:
                                first_part(prep, "qk"[layer])
                            if n == 3:
                                second_part(prep, "kq"[layer])
                            if n == 4:
                                second_part(prep, "qk"[layer])
                        if n == 5 and layer == 0 and done is not None:
                            result_apply(done)
                        if n == 4 and layer == 1 and done is not None:
                            att_turned(done)
                        if n == MAX_T[layer] and mxc is not None:
                            maxT(mxc)
                        if n == 7 and layer == 0 and done is not None:
                            z_turned(done)
                        if n >= 2 and n % 2 == 0:
                            p = n // 2 - 1
                            act.wait_ge(av_ps, g + (2 * p + 2))
                            if after(att_c.n * NP + (p - 1)):
                                act.wait_ge(avT_ps, att_c.n * NP + (p - 1))
                            nc.scalar.copy(av_sb[p % 2][:], av[p % 2][:, 0:256]).then_inc(av_ok, 1)
                        if n == 8 and layer == 0 and ahead is not None:
                            ahead_apply(ahead)
                    if prep is not None:
                        values(prep)

                def last(c):
                    if layer == 0:
                        result_apply(c)
                        z_turned(c)
                    else:
                        att_turned(c)
                walk(act, layer, first, step, last)
                if layer == 0:
                    act.wait_ge(g_pe, 1)
                    nc.scalar.activation(hid[0:GH, :], s1[0][0:GH, 0:B], ACT.Relu, bias=gb1_c[:]).then_inc(g_act, 1)
                    act.wait_ge(g_dve, 4)
                    nc.scalar.activation(ex[:], lg[:], ACT.Exp, bias=nmax[:]).then_inc(g_act, 1)

        @block.vector
        def _(dve):
            def clear_stack(k):
                nc.vector.memset(kbd[k][:].rearrange("r h t p -> r (h t p)").bitcast(f32), 0.0).then_inc(c_kbd, 1)

            def clear_av():
                for k in range(2):
                    nc.vector.memset(av[k][:], 0.0).then_inc(c_av, 1)
                nc.vector.memset(hid[GH:GH + 1, :], 1.0).then_inc(c_av, 1)

            def ahead_stats(c):
                dve.wait_ge(d_x[c.k], c.u * 16 + 16)
                if after(c.c):
                    dve.wait_ge(ln_rs, c.c)
                for p in range(NP):
                    nc.vector.bn_stats(stats[:, p, :], x1[:, bass.ds(c.c * NP + p, 1), :])
                dve.drain()
                for p in range(NP):
                    nc.vector.bn_aggr(mv[:, p, :], stats[:, p, :]).then_inc(ln_mv, 1)

            def result_stats(c):
                dve.wait_ge(add_ok, c.c * NP + NP)
                if after(c.c):
                    dve.wait_ge(l2_rs, c.c)
                for p in range(NP):
                    nc.vector.bn_stats(stats2[:, p, :], x1[:, bass.ds(c.c * NP + p, 1), :])
                dve.drain()
                for p in range(NP):
                    nc.vector.bn_aggr(mv2[:, p, :], stats2[:, p, :]).then_inc(l2_mv, 1)

            def pool_tokens(c):
                dve.wait_ge(zT_ok, c.c + 1)
                nc.vector.tensor_reduce(pooled[:, bass.ds(c.c * 2 * NP, 2 * NP)],
                                        zT[:, bass.ds(c.c * TOK, TOK)].rearrange("f (b t) -> f b t", t=S),
                                        AX.X, ALU.add).then_inc(pool_ok, 1)

            def rest(c, which):
                if which == "q":
                    ps, hi, rs, lo, part, first, dst, bias, view = (
                        pa[c.layer], q_hi, q_r, q_lo, qpart, 0, q_rest, qbs_c, "f (b p t) -> f p b t")
                else:
                    ps, hi, rs, lo, part, first, dst, bias, view = (
                        pa[1 - c.layer], k_hi, k_r, k_lo, kpart, 2, k_rest, kb_c, "f (b t p) -> f p b t")
                dve.wait_ge(hi, c.n + 1)
                if after(c.n):
                    dve.wait_ge(lo, c.n)
                for b in range(2):
                    last = nc.vector.scalar_tensor_tensor(out=dst[:].rearrange(view, b=2, p=NP)[:, :, b],
                                                          in0=ps[:].rearrange("f (p b t) -> f p b t", p=NP, b=2)[:, :, b],
                                                          scalar=bias[:] if c.layer else 0.0,
                                                          in1=part[c.k][:, first, :].rearrange(view, b=2, p=NP)[:, :, b],
                                                          op0=ALU.add if c.layer else ALU.max, op1=ALU.subtract)
                last.then_inc(rs, 1)

            def gate_rank(c, p, bank):
                dve.wait_ge(xv_ps[p], c.c + 1)
                if p == "v" or p == "q" or p == "k":
                    used = {"q": q_ps, "k": k_ps, "v": v_ps}[p]
                    if after(c.c):
                        dve.wait_ge(used, c.n)
                elif after(c.c):
                    dve.wait_ge(o_ps, c.c)
                nc.vector.tensor_tensor(xvs[p][:].rearrange("e (b t) -> e b t", t=S), bank[:].rearrange("e (b t) -> e b t", t=S),
                                        sg[p][:, bass.ds(c.c * 2 * NP, 2 * NP)].rearrange("e (b o) -> e b o", o=1).broadcast_to([128, 2 * NP, S]),
                                        ALU.mult).then_inc(xv_ok[p], 1)

            def maxima(c, unit):
                p, g = unit // 2, unit % 2
                dve.wait_ge(sc_ps, c.n * 8 + (unit + 1))
                nc.vector.tensor_reduce(mx[:, 2 * g:2 * g + 2, :].rearrange("q b (g p) -> q g b p", p=NP)[:, :, :, p],
                                        s1[unit % 2][:].rearrange("q (g b k) -> q g b k", g=4, b=2),
                                        AX.X, ALU.max).then_inc(max_ok, 1)

            def max_parts(c):
                dve.wait_ge(max_ok, c.n * 8 + 8)
                if after(c.n):
                    dve.wait_ge(mT_pe, c.n)
                nc.vector.tensor_scalar(mxp[:, :, 0, :], mx[:], -1.0, None, ALU.mult).then_inc(m_hi, 1)
                dve.wait_ge(m_hi, c.n + 1)
                nc.vector.scalar_tensor_tensor(out=mx_rest[:], in0=mx[:], scalar=-1.0, in1=mxp[:, :, 0, :],
                                               op0=ALU.mult, op1=ALU.subtract).then_inc(m_r, 1)
                dve.wait_ge(m_r, c.n + 1)
                nc.vector.tensor_copy(mxp[:, :, 1, :], mx_rest[:]).then_inc(m_mid, 1)
                dve.wait_ge(m_mid, c.n + 1)
                nc.vector.tensor_tensor(mxp[:, :, 2, :], mx_rest[:], mxp[:, :, 1, :], ALU.subtract).then_inc(m_parts, 1)

            def divide(c, p):
                j = c.n * NP + (p + 1)
                dve.wait_ge(avT_ps, j)
                vw = av[p % 2][:, 256:512].rearrange("q (g w) -> q g w", w=32)
                nc.vector.reciprocal(rden[:, p % 2], vw[:, :, DH:2 * VW:VW]).then_inc(rden_ok, 1)
                dve.wait_ge(rden_ok, j)
                if c.layer == 0 and after((c.n - 2) * NP + (p + 1)):
                    dve.wait_ge(add_ok, (c.n - 2) * NP + (p + 1))
                if c.layer == 1 and after(c.c - 1):
                    dve.wait_ge(aT_ps, c.c - 1)
                for hp in range(2):
                    for b in range(2):
                        q0 = S * hp
                        last = nc.vector.tensor_tensor(
                            att[c.k][S * b:S * b + S, p, :].rearrange("q (s e c d) -> q s e c d", s=2, e=2, c=4)[:, :, hp],
                            vw[q0:q0 + S, :, VW * b:VW * b + DH].rearrange("q (s c) d -> q s c d", s=2),
                            rden[q0:q0 + S, p % 2, :, b:b + 1].rearrange("q (s c) o -> q s c o", s=2).broadcast_to([S, 2, 4, DH]), ALU.mult)
                last.then_inc(att_ok, 1)

            def values(c):
                if c.layer == 1:
                    dve.wait_ge(v_ps, c.n + 1)
                    if after((c.n - 1) * 8):
                        dve.wait_ge(av_ps, (c.n - 1) * 8)
                    for b in range(2):
                        last = nc.vector.tensor_tensor(
                            vbd[c.k][S * b:S * b + S, :, :, VW * b:VW * b + DH],
                            pa[0][S * b:S * b + S, :].rearrange("t (p h d) -> t p h d", p=NP, h=H),
                            vb_bc[S * b:S * b + S, :].rearrange("t (o h d) -> t o h d", o=1, h=H).broadcast_to([S, NP, H, DH]), ALU.add)
                    last.then_inc(v_ok, 1)

            def result(c):
                dve.wait_ge(o_ps, c.c + 1)
                dve.wait_ge(xo_ok, c.c + 1)
                if after((c.c - 1)):
                    dve.wait_ge(d_out[c.k], (c.u - NC // 2) * 16)
                nc.vector.tensor_tensor(osb[c.k][:].rearrange("t p f -> t (p f)"), pa[1][:],
                                        xo[:].rearrange("t p f -> t (p f)"), ALU.add).then_inc(o_ok, 1)

            for layer in range(2):
                def first(ch):
                    if layer == 0:
                        ahead_stats(ch(0, 0))
                        clear_stack(0)
                        ahead_stats(ch(0, 1))
                    for j in range(2):
                        c = ch(0, j)
                        if layer == 0:
                            rest(c, "k")
                            rest(c, "q")
                            if j == 0:
                                clear_stack(1)
                        else:
                            gate_rank(c, "q", pa[1])
                            gate_rank(c, "k", pa[0])
                            rest(c, "q")
                            rest(c, "k")
                            gate_rank(c, "v", pa[0])
                            values(c)
                    if layer == 0:
                        clear_av()
                        dve.wait_ge(c_set, 5)
                        nc.vector.tensor_reduce(pick_of[:], ident[0:2 * PARTS * GP, 0:2 * PARTS * GP].rearrange(
                            "r (b s i) -> r b i s", b=2, s=PARTS), AX.X, ALU.add).then_inc(c_pick, 1)
                        dve.wait_ge(c_pick, 1)
                        nc.vector.tensor_copy(pick[:].rearrange("r i (b t) -> r i b t", b=2),
                                              pick_of[:].rearrange("r b (i o) -> r i b o", o=1).broadcast_to(
                                                  [2 * PARTS * GP, GP, 2, S])).then_inc(c_pick, 1)
                        ahead_stats(ch(0, 2))
                    for u in range(8):
                        maxima(ch(0, 0), u)
                    max_parts(ch(0, 0))

                def step(prep, mxc, att_c, done, ahead):
                    for n in range(10):
                        if mxc is not None:
                            for unit in UNITS[layer].get(n, ()):
                                maxima(mxc, unit)
                            if n == LAST_UNITS[layer]:
                                max_parts(mxc)
                        if layer == 0:
                            if n == 0 and done is not None:
                                result_stats(done)
                            if n == 1 and prep is not None:
                                rest(prep, "k")
                            if n == 2 and prep is not None:
                                rest(prep, "q")
                        else:
                            if prep is not None:
                                if n == 0:
                                    gate_rank(prep, "q", pa[1])
                                    gate_rank(prep, "k", pa[0])
                                if n == 1:
                                    rest(prep, "q")
                                if n == 2:
                                    rest(prep, "k")
                            if n == 4 and done is not None:
                                gate_rank(done, "o", pa[1])
                        if n == 5 and layer == 1 and prep is not None:
                            gate_rank(prep, "v", pa[0])
                        if n == 5 and layer == 0 and ahead is not None:
                            ahead_stats(ahead)
                        if n == 8 and layer == 0 and done is not None:
                            pool_tokens(done)
                        if n == 7 and layer == 1 and done is not None:
                            result(done)
                        if n == 9 and layer == 1 and prep is not None:
                            values(prep)
                        if n >= 3 and n % 2 == 1:
                            divide(att_c, (n - 3) // 2)

                def last(c):
                    if layer == 0:
                        result_stats(c)
                        pool_tokens(c)
                    else:
                        gate_rank(c, "o", pa[1])
                        result(c)
                walk(dve, layer, first, step, last)

                if layer == 0:
                    dve.wait_ge(g_pe, 2)
                    nc.vector.tensor_copy(lg[:], s1[1][:, 0:E]).then_inc(g_dve, 1)
                    dve.wait_ge(g_dve, 1)
                    dve.wait_ge(c_tri, 3)
                    dve.wait_ge(d_vec, 12 * 16)
                    other = lg[:].rearrange("b (o e) -> b o e", o=1).broadcast_to([128, E, E])
                    own = lg[:].rearrange("b (e o) -> b e o", o=1).broadcast_to([128, E, E])
                    nc.vector.tensor_tensor(beat[:], other, own, ALU.is_gt).then_inc(g_dve, 1)
                    nc.vector.tensor_tensor(tie[:], other, own, ALU.is_equal).then_inc(g_dve, 1)
                    nc.vector.tensor_reduce(nmax[:], lg[:], AX.X, ALU.max, negate=True).then_inc(g_dve, 1)
                    dve.wait_ge(g_dve, 4)
                    nc.vector.tensor_tensor(tie[:], tie[:], tri[:], ALU.mult).then_inc(g_dve, 1)
                    dve.wait_ge(g_dve, 5)
                    nc.vector.tensor_tensor(beat[:], beat[:], tie[:], ALU.add).then_inc(g_dve, 1)
                    dve.wait_ge(g_dve, 6)
                    nc.vector.tensor_reduce(rank[:], beat[:], AX.X, ALU.add).then_inc(g_dve, 1)
                    dve.wait_ge(g_dve, 7)
                    dve.wait_ge(g_act, 2)
                    nc.vector.scalar_tensor_tensor(out=ex[:], in0=rank[:], scalar=1.5, in1=ex[:],
                                                   op0=ALU.is_lt, op1=ALU.mult).then_inc(g_dve, 1)
                    dve.wait_ge(g_dve, 8)
                    nc.vector.tensor_reduce(gsum[:], ex[:], AX.X, ALU.add).then_inc(g_dve, 1)
                    dve.wait_ge(g_dve, 9)
                    nc.vector.reciprocal(rsum[:], gsum[:]).then_inc(g_dve, 1)
                    dve.wait_ge(g_dve, 10)
                    nc.vector.tensor_scalar(gexp[:], ex[:].rearrange("b (e o) -> b e o", o=1).broadcast_to([128, E, R]),
                                            rsum[:], None, ALU.mult).then_inc(g_dve, 1)
                    dve.wait_ge(g_pe, 3)
                    for j, p in enumerate("qkvo"):
                        nc.vector.tensor_scalar(sg[p][:], s1[0][:, 0:B], s_col[:, j:j + 1], None, ALU.mult).then_inc(g_dve, 1)
                    dve.wait_ge(g_dve, 15)

        @block.tensor
        def _(pe):
            def turn_weights(names):
                for n in names:
                    if n >= 2 and n != 3:
                        pe.wait_ge(w_done, n - 1)
                    nc.tensor.transpose(pa[n % 2][:, 0:128], w_nat[:, n, :], ident[:]).then_inc(w_ps, 1)

            def W(name):
                return wT[:, WI[name], :]

            def turn_ctx(c):
                pe.wait_ge(d_ctx[c.k], c.u * 16 + 16)
                if after(c.n):
                    pe.wait_ge(k_r, c.n)
                if after(c.c - 3):
                    pe.wait_ge(zT_ok, c.c - 3)
                for p in range(NP):
                    last = nc.tensor.transpose(pa[1][:, 128 * p:128 * p + 128], ctx_sb[c.k][:, p, :], ident[:])
                last.then_inc(cT_ps, 1)

            def turn_x(c):
                pe.wait_ge(ln_x, c.c * NP + NP)
                if after(c.n):
                    pe.wait_ge(v_ok, c.n)
                for p in range(NP):
                    last = nc.tensor.transpose(pa[0][:, 128 * p:128 * p + 128], xn[c.k][:, p, :], ident[:])
                last.then_inc(xT_ps, 1)

            def cross_keys(c):
                pe.wait_ge(cT_ok, c.c + 1)
                nc.tensor.matmul(pa[1][:], W("wk"), cT[:], start=True, stop=True).then_inc(k_ps, 1)

            def cross_queries(c):
                pe.wait_ge(xT_ok, c.c + 1)
                nc.tensor.matmul(pa[0][:], W("wq"), fT[:], start=True, stop=True).then_inc(q_ps, 1)

            def turn_z(c, prep):
                pe.wait_ge(l2_z, c.c * NP + NP)
                if prep is not None:
                    pe.wait_ge(k_r, prep.n + 1)
                elif after(c.c):
                    pe.wait_ge(k_r, NC)
                    pe.wait_ge(zT_ok, c.c)
                for p in range(NP):
                    last = nc.tensor.transpose(pa[1][:, 128 * p:128 * p + 128], z[:, p, :], ident[:])
                last.then_inc(zT_ps, 1)

            def query_ranks(c):
                pe.wait_ge(f_ok, c.c + 1)
                pe.wait_ge(q_r, c.n)
                if after(c.c - 3):
                    pe.wait_ge(o_ok, c.c - 3)
                nc.tensor.matmul(pa[1][:], W("qV"), cT[:], start=True, stop=True).then_inc(xv_ps["q"], 1)

            def key_ranks(c):
                pe.wait_ge(v_ok, c.n)
                nc.tensor.matmul(pa[0][:], W("kV"), cT[:], start=True, stop=True).then_inc(xv_ps["k"], 1)

            def project(c, p, bank, done):
                pe.wait_ge(xv_ok[p], c.c + 1)
                nc.tensor.matmul(bank[:], W(p + "W"), cT[:], start=True, stop=False)
                nc.tensor.matmul(bank[:], W(p + "U"), xvs[p][:], start=False, stop=True).then_inc(done, 1)

            def value_ranks(c):
                pe.wait_ge(k_r, c.n + 1)
                nc.tensor.matmul(pa[0][:], W("vV"), cT[:], start=True, stop=True).then_inc(xv_ps["v"], 1)

            def turn_att(c, prep):
                pe.wait_ge(att_ok, c.n * NP + NP)
                if prep is not None:
                    pe.wait_ge(q_r, prep.n + 1)
                else:
                    pe.wait_ge(q_r, 2 * NC)
                    pe.wait_ge(o_ok, c.c)
                for p in range(NP):
                    last = nc.tensor.transpose(pa[1][:, 128 * p:128 * p + 128], att[c.k][:, p, :], ident[:])
                last.then_inc(aT_ps, 1)

            def output_ranks(c):
                pe.wait_ge(aT_ok, c.c + 1)
                nc.tensor.matmul(pa[1][:], W("oV"), attT[:], start=True, stop=True).then_inc(xv_ps["o"], 1)

            def output(c):
                pe.wait_ge(xv_ok["o"], c.c + 1)
                for p in range(NP):
                    cols = slice(128 * p, 128 * p + 128)
                    nc.tensor.matmul(pa[1][:, cols], attT[:, cols], W("oW"), start=True, stop=False)
                    last = nc.tensor.matmul(pa[1][:, cols], xvs["o"][:, cols], W("oU"), start=False, stop=True)
                last.then_inc(o_ps, 1)

            def values(c):
                if c.layer == 0:
                    pe.wait_ge(q_r, c.n + 1)
                else:
                    pe.wait_ge(xv_ok["v"], c.c + 1)
                for p in range(NP):
                    cols = slice(128 * p, 128 * p + 128)
                    if c.layer == 0:
                        last = nc.tensor.matmul(pa[0][:, cols], cT[:, cols], W("wv"), start=True, stop=True)
                    else:
                        nc.tensor.matmul(pa[0][:, cols], cT[:, cols], W("vW"), start=True, stop=False)
                        last = nc.tensor.matmul(pa[0][:, cols], xvs["v"][:, cols], W("vU"), start=False, stop=True)
                last.then_inc(v_ps, 1)

            def scores(c, unit):
                p, g = unit // 2, unit % 2
                if unit == 0:
                    pe.wait_ge(d_qget[c.k], c.u * 16 + 16)
                    pe.wait_ge(d_kget[c.k], c.u * 32 + 32)
                    if after(c.n):
                        pe.wait_ge(mT_ok, c.n)
                if after(c.n * 8 + (unit - 1)):
                    pe.wait_ge(max_ok, c.n * 8 + (unit - 1))
                for j in range(4):
                    for a in range(2):
                        h = 2 * (4 * g + j) + a
                        last = nc.tensor.matmul(s1[unit % 2][S * a:S * a + S, 128 * j:128 * j + 128],
                                                qst[c.k][0:ROWS, h, p, :], kbd[c.k][0:ROWS, h, :, p], start=True, stop=True)
                last.then_inc(sc_ps, 1)

            def maxT(c):
                pe.wait_ge(m_parts, c.n + 1)
                for half in range(2):
                    last = nc.tensor.transpose(mT_ps[0:2 * PARTS * GP, half, :],
                                               mxp[:, 2 * half:2 * half + 2].rearrange("q b s i -> q (b s i)"), identb[:])
                last.then_inc(mT_pe, 1)

            def shifted(c, n):
                p, half = n // 2, n % 2
                if n == 0:
                    pe.wait_ge(mT_ok, c.n + 1)
                if after(c.n * 8 + (n - 1)):
                    pe.wait_ge(exp_ok, c.n * 8 + (n - 1))
                for g in range(UNIT_H // 2):
                    nc.tensor.matmul(s2[n % 2][:, 2 * S * g:2 * S * g + 2 * S], pick[:, NP * g + p, :], mxT[c.k][:, half, :],
                                     start=True, stop=False)
                    for j in range(2 * g, 2 * g + 2):
                        h = UNIT_H * half + j
                        last = nc.tensor.matmul(s2[n % 2][:, S * j:S * j + S], kbd[c.k][:, h, :, p], qst[c.k][:, h, p, :],
                                                start=False, stop=j % 2 == 1)
                last.then_inc(s2_ps, 1)

            def times_values(c, n):
                p, half = n // 2, n % 2
                pe.wait_ge(exp_ok, c.n * 8 + (n + 1))
                if n == 0:
                    pe.wait_ge(v_ok, c.n + 1)
                if half == 0 and after(c.n * NP + (p - 1)):
                    pe.wait_ge(att_ok, c.n * NP + (p - 1))
                for j in range(8):
                    h = 8 * half + j
                    g = h // 4
                    last = nc.tensor.matmul(av[p % 2][32 * (h % 4):32 * (h % 4) + 2 * VW, S * g:S * g + S],
                                            vbd[c.k][:, p, h, :], prob[n % 4][:, j, :], start=True, stop=True)
                last.then_inc(av_ps, 1)

            def turn(c, p):
                pe.wait_ge(av_ok, c.n * NP + (p + 1))
                for s in range(2):
                    last = nc.tensor.transpose(av[p % 2][:, 256 + 128 * s:384 + 128 * s],
                                               av_sb[p % 2][:, 128 * s:128 * s + 128], ident[:])
                last.then_inc(avT_ps, 1)

            for layer in range(2):
                def first(ch):
                    if layer == 0:
                        pe.wait_ge(c_set, 5)
                        pe.wait_ge(d_w3, 48)
                        turn_weights(range(3))
                        pe.wait_ge(w_done, 3)
                    for j in range(2):
                        c = ch(0, j)
                        if layer == 0:
                            turn_ctx(c)
                            turn_x(c)
                            cross_keys(c)
                            cross_queries(c)
                        else:
                            query_ranks(c)
                            key_ranks(c)
                            project(c, "q", pa[1], q_ps)
                            project(c, "k", pa[0], k_ps)
                            value_ranks(c)
                        values(c)
                    if layer == 0:
                        pe.wait_ge(v_ok, 2)
                        pe.wait_ge(k_r, 2)
                        pe.wait_ge(d_w, 16 * (NW - 3))
                        turn_weights(range(3, NW))
                        pe.wait_ge(w_done, NW - 1)
                        pe.wait_ge(d_vec, 12 * 16)
                        nc.tensor.transpose(pa[NW % 2][:, 0:GH], gw1_nat[:], ident[0:GH, 0:GH]).then_inc(w_ps, 1)
                        pe.wait_ge(c_tri, 1)
                    for u in range(8):
                        scores(ch(0, 0), u)
                    maxT(ch(0, 0))
                    if layer == 0:
                        pe.wait_ge(w_done, NW + 2)
                        pe.wait_ge(c_av, 2)
                        pe.wait_ge(c_pick, 2)

                def step(prep, mxc, att_c, done, ahead):
                    if layer == 0 and prep is not None:
                        turn_ctx(prep)
                    for n in range(10):
                        if n < 8:
                            shifted(att_c, n)
                        if prep is not None:
                            if n == 0:
                                if layer == 1:
                                    query_ranks(prep)
                                    key_ranks(prep)
                            if n == 1:
                                if layer == 0:
                                    turn_x(prep)
                                    cross_keys(prep)
                                else:
                                    project(prep, "q", pa[1], q_ps)
                            if n == 2:
                                if layer == 0:
                                    cross_queries(prep)
                                else:
                                    project(prep, "k", pa[0], k_ps)
                        if mxc is not None:
                            for unit in UNITS[layer].get(n, ()):
                                scores(mxc, unit)
                        if n == MAX_T[layer] and mxc is not None:
                            maxT(mxc)
                        if n == 7 and layer == 0 and done is not None:
                            turn_z(done, prep)
                        if n == 4 and layer == 1:
                            if prep is not None:
                                value_ranks(prep)
                        if 1 <= n <= 8:
                            times_values(att_c, n - 1)
                        if layer == 1 and done is not None:
                            if n == 3:
                                turn_att(done, prep)
                            if n == 4:
                                output_ranks(done)
                            if n == 6:
                                output(done)
                        if prep is not None and n == (9, 6)[layer]:
                            values(prep)
                        if n >= 3 and n % 2 == 1:
                            turn(att_c, (n - 3) // 2)

                def last(c):
                    if layer == 0:
                        turn_z(c, None)
                    else:
                        turn_att(c, None)
                        output_ranks(c)
                        output(c)
                walk(pe, layer, first, step, last)
                if layer == 0:
                    pe.wait_ge(pool_ok, NC)
                    pe.wait_ge(c_av, 3)
                    pe.wait_ge(mT_ok, NC)
                    pe.wait_ge(max_ok, 8 * NC)
                    nc.tensor.matmul(s1[0][0:GH, 0:B], gw1T[:], pooled[:], start=True, stop=True).then_inc(g_pe, 1)
                    pe.wait_ge(g_act, 1)
                    nc.tensor.matmul(s1[1][:, 0:E], hid[:], gw2T[:], start=True, stop=True).then_inc(g_pe, 1)
                    pe.wait_ge(g_dve, 11)
                    nc.tensor.transpose(s1[0][:, 0:B], gexp[:].rearrange("b e r -> b (e r)"), ident[:]).then_inc(g_pe, 1)
                    pe.wait_ge(g_dve, 15)


_P = ("Wm", "U", "S", "V", "b")
_INS = (["x", "ctx_1024", "L0_xattn_Wq", "L0_xattn_Wk", "L0_xattn_Wv",
         "L0_ffn_gw1", "L0_ffn_gb1", "L0_ffn_gw2", "L0_ffn_gb2"]
        + ["L0_ffn_" + p + s for p in "qkvo" for s in _P])
_OUTS = [((B, S, D), 'float32')]


def kernel(**inputs):
    import numpy as _np
    import concourse.bacc as _bacc
    from concourse import mybir as _mybir
    from concourse.bass_utils import run_bass_kernel_spmd as _run

    nc = _bacc.Bacc("TRN2", target_bir_lowering=False, num_devices=1)
    arrays, args = {}, []
    for name in _INS:
        a = _np.ascontiguousarray(inputs[name])
        arrays[f"in_{name}_dram"] = a
        args.append(nc.dram_tensor(f"in_{name}_dram", a.shape, _mybir.dt.from_np(a.dtype), kind="ExternalInput").ap())
    for i, (shape, dtype) in enumerate(_OUTS):
        dt = _mybir.dt.from_np(_np.dtype(dtype))
        args.append(nc.dram_tensor(f"out_{i}_dram", shape, dt, kind="ExternalOutput").ap())
    xattn_ffn_kernel(nc, *args)
    r = _run(nc, [arrays], core_ids=[0])
    got = tuple(r.results[0][f"out_{i}_dram"] for i in range(len(_OUTS)))
    return got[0]
```

```python
import concourse.bass as bass
from concourse import mybir
from contextlib import ExitStack


B, S, D = 128, 64, 128
H, DH = 16, 8
E, R, GH = 8, 16, 32
NP = 4
TOK = NP * 2 * S
NC = B // (2 * NP)
EPS = 1e-5
SCALE = DH ** -0.5
PARTS = 3
SLOTS = 6
ROWS = 2 * SLOTS * DH
UNIT_H = H // 2
VW = DH + 1


class Chunk:

    def __init__(self, layer, it, off):
        self.layer = layer
        self.c = it * 2 + off
        self.n = it * 2 + (off + NC * layer)
        self.k = off % 2
        self.u = it + (off // 2 + NC // 2 * layer)


def after(value):
    return not isinstance(value, int) or value > 0


def xattn_ffn_kernel(nc, x, ctx_in, wq, wk, wv, gw1, gb1, gw2, gb2,
                     qWm, qU, qS, qV, qb, kWm, kU, kS, kV, kb,
                     vWm, vU, vS, vV, vb, oWm, oU, oS, oV, ob, out):
    f32, bf16 = mybir.dt.float32, mybir.dt.bfloat16
    ALU, ACT, AX = mybir.AluOpType, mybir.ActivationFunctionType, mybir.AxisListType

    x_d = x.rearrange("(p b) t f -> (b t) p f", b=2)
    c_d = ctx_in.rearrange("(p b) t f -> (b t) p f", b=2)
    o_d = out.rearrange("(p b) t f -> (b t) p f", b=2)

    qpd = [nc.dram_tensor(f"q_parts_dram{k}", [H, DH, SLOTS, TOK], bf16, kind="Internal").ap() for k in range(2)]
    kpd = [nc.dram_tensor(f"k_parts_dram{k}", [H, DH, SLOTS, TOK], bf16, kind="Internal").ap() for k in range(2)]

    NAMES = ["wq", "wk", "wv", "qW", "kW", "vW", "oW", "qV", "kV", "vV", "oV", "qU", "kU", "vU", "oU"]
    NW = len(NAMES)
    SCALED = ("wq", "qW", "qU")
    WI = {n: i for i, n in enumerate(NAMES)}
    w_src = dict(wq=wq, wk=wk, wv=wv, qW=qWm, kW=kWm, vW=vWm, oW=oWm)
    for n, v in (("qV", qV), ("kV", kV), ("vV", vV), ("oV", oV)):
        w_src[n] = v.rearrange("e r d -> (e r) d")
    u_src = dict(qU=qU, kU=kU, vU=vU, oU=oU)

    with ExitStack() as st:
        def sb(name, shape, dt=f32):
            return st.enter_context(nc.sbuf_tensor(name, shape, dt))

        def sem(name):
            return st.enter_context(nc.semaphore(name))

        def sem2(name):
            return [sem(f"{name}{k}") for k in range(2)]

        x1 = sb("x1", [128, NC * NP, D])
        zT = sb("zT", [128, NC * TOK])
        kbd = [sb(f"kbd{k}", [ROWS, H, 2 * S, NP], bf16) for k in range(2)]
        qst = [sb(f"qst{k}", [ROWS, H, NP, S], bf16) for k in range(2)]
        w_nat = zT[:, 0:NW * D].rearrange("p (n f) -> p n f", n=NW)
        prob = [sb(f"prob{j}", [128, 8, S]) for j in range(4)]
        vbd = [sb(f"vbd{k}", [128, NP, H, 2 * VW]) for k in range(2)]
        wT = sb("wT", [128, NW, D])
        ident = sb("ident", [128, 128])
        identb = sb("identb", [128, 128], bf16)
        ctx_sb = [sb(f"ctx_sb{k}", [128, NP, D]) for k in range(2)]
        xn = [sb(f"xn{k}", [128, NP, D]) for k in range(2)]
        z = sb("z", [128, NP, D])
        fT = sb("fT", [128, TOK])
        cT = sb("cT", [128, TOK])
        qpart = [sb(f"qpart{k}", [128, PARTS, TOK], bf16) for k in range(2)]
        kpart = [sb(f"kpart{k}", [128, PARTS, TOK], bf16) for k in range(2)]
        q_rest = sb("q_rest", [128, TOK])
        k_rest = sb("k_rest", [128, TOK])
        GP = UNIT_H // 2 * NP
        mx = sb("mx", [128, 4, GP])
        mxp = sb("mxp", [128, 4, PARTS, GP], bf16)
        mx_rest = sb("mx_rest", [128, 4, GP])
        mxT = [sb(f"mxT{k}", [2 * PARTS * GP, 2, 128], bf16) for k in range(2)]
        pick_of = sb("pick_of", [2 * PARTS * GP, 2, GP])
        pick = sb("pick", [2 * PARTS * GP, GP, 2 * S], bf16)
        av_sb = [sb(f"av_sb{j}", [128, 256]) for j in range(2)]
        rden = sb("rden", [128, 2, 8, 2])
        att = [sb(f"att{k}", [128, NP, D]) for k in range(2)]
        stats = sb("stats", [128, NP, 6])
        mv = sb("mv", [128, NP, 2])
        rstd = sb("rstd", [128, NP])
        m_half = sb("m_half", [128, NP])
        eps_c = sb("eps_c", [128, NP])
        stats2 = sb("stats2", [128, NP, 6])
        mv2 = sb("mv2", [128, NP, 2])
        rstd2 = sb("rstd2", [128, NP])
        shift = sb("shift", [128, NP])
        shift2 = sb("shift2", [128, NP])
        m_one = sb("m_one", [128, NP])
        xvs = {p: sb("xvs_" + p, [128, TOK]) for p in "vo"}
        for k, p in enumerate("qk"):
            xvs[p] = xn[k][:].rearrange("e p f -> e (p f)")
        attT, xo, osb = fT, z, ctx_sb
        vb_bc = sb("vb_bc", [128, D])
        ob_bc = sb("ob_bc", [128, D])
        qb_c = sb("qb_c", [128, 1])
        qbs_c = sb("qbs_c", [128, 1])
        kb_c = sb("kb_c", [128, 1])
        s_col = sb("s_col", [128, 4])
        gw1_nat = sb("gw1_nat", [GH, D])
        gw1T = sb("gw1T", [128, GH])
        gb1_c = sb("gb1_c", [GH, 1])
        gw2T = sb("gw2T", [GH + 1, E])
        hid = sb("hid", [GH + 1, B])
        pooled = sb("pooled", [128, B])
        lg = sb("lg", [128, E])
        tri = sb("tri", [128, E, E])
        beat = sb("beat", [128, E, E])
        tie = sb("tie", [128, E, E])
        rank = sb("rank", [128, E])
        nmax = sb("nmax", [128, 1])
        ex = sb("ex", [128, E])
        gsum = sb("gsum", [128, 1])
        rsum = sb("rsum", [128, 1])
        gexp = sb("gexp", [128, E, R])
        sg = {p: sb("sg_" + p, [128, B]) for p in "qkvo"}

        def pb(name):
            return st.enter_context(nc.psum_tensor(name, [128, 512], f32))
        s1 = [pb(f"ps_s1_{j}") for j in range(2)]
        s2 = [pb(f"ps_s2_{j}") for j in range(2)]
        av = [pb(f"ps_av_{j}") for j in range(2)]
        pa = [pb(f"ps_a_{j}") for j in range(2)]
        mT_ps = s1[0][:, 0:128].bitcast(bf16).rearrange("p (b c) -> p b c", b=2)

        d_w3, d_w, d_vec = sem("d_w3"), sem("d_w"), sem("d_vec")
        d_x, d_ctx = sem2("d_x"), sem2("d_ctx")
        d_qput, d_kput = sem2("d_qput"), sem2("d_kput")
        d_qget, d_kget = sem2("d_qget"), sem2("d_kget")
        d_out = sem2("d_out")
        c_set = sem("c_set")
        c_tri = sem("c_tri")
        c_vbd, c_kbd, c_av = sem("c_vbd"), sem("c_kbd"), sem("c_av")
        c_pick = sem("c_pick")
        w_ps, w_done = sem("w_ps"), sem("w_done")
        ln_mv, ln_rs, ln_x = sem("ln_mv"), sem("ln_rs"), sem("ln_x")
        l2_mv, l2_rs, l2_z = sem("l2_mv"), sem("l2_rs"), sem("l2_z")
        xT_ps, xT_ok, cT_ps, cT_ok = sem("xT_ps"), sem("xT_ok"), sem("cT_ps"), sem("cT_ok")
        ln_ve, l2_ve = sem("ln_ve"), sem("l2_ve")
        zT_ps, zT_ok, pool_ok = sem("zT_ps"), sem("zT_ok"), sem("pool_ok")
        q_ps, q_hi, q_r, q_mid, q_lo = sem("q_ps"), sem("q_hi"), sem("q_r"), sem("q_mid"), sem("q_lo")
        k_ps, k_hi, k_r, k_mid, k_lo = sem("k_ps"), sem("k_hi"), sem("k_r"), sem("k_mid"), sem("k_lo")
        v_ps, v_ok = sem("v_ps"), sem("v_ok")
        sc_ps, max_ok = sem("sc_ps"), sem("max_ok")
        m_hi, m_r, m_mid, m_parts = sem("m_hi"), sem("m_r"), sem("m_mid"), sem("m_parts")
        mT_pe, mT_ok = sem("mT_pe"), sem("mT_ok")
        s2_ps, exp_ok, av_ps, av_ok, avT_ps = sem("s2_ps"), sem("exp_ok"), sem("av_ps"), sem("av_ok"), sem("avT_ps")
        rden_ok, att_ok, add_ok = sem("rden_ok"), sem("att_ok"), sem("add_ok")
        xv_ps = {p: sem("xv_ps_" + p) for p in "qkvo"}
        xv_ok = {p: sem("xv_ok_" + p) for p in "qkvo"}
        f_ok = sem("f_ok")
        aT_ps, aT_ok, o_ps, o_ok, xo_ok = sem("aT_ps"), sem("aT_ok"), sem("o_ps"), sem("o_ok"), sem("xo_ok")
        g_pe, g_act, g_dve = sem("g_pe"), sem("g_act"), sem("g_dve")

        block = st.enter_context(nc.Block())

        UNITS = ({1: (0, 1), 2: (2, 3), 3: (4, 5), 4: (6, 7)}, {3: (0, 1), 4: (2, 3), 5: (4, 5), 6: (6, 7)})
        LAST_UNITS = (4, 6)
        MAX_T = (7, 7)

        def walk(eng, layer, step, first=None, gate=None, normed=None, turned=None, last=None):
            ch = lambda it, off: Chunk(layer, it, off)

            def chunk(i):
                if i < NC:
                    return Chunk(layer, 0, i)
                return Chunk(1, 0, i - NC) if layer == 0 else None

            def single(i):
                step(chunk(i + 2), chunk(i + 1), chunk(i), chunk(i - 1) if i else None, chunk(i + 3))
            if first is not None:
                first(ch)
            single(0)
            if layer == 1:
                if turned is not None:
                    turned(Chunk(0, 0, NC - 1))
                if gate is not None:
                    gate(1)
            single(1)
            looped = NC - 4
            with eng.Fori(1, looped // 2) as it:
                for k in range(2):
                    step(ch(it, k + 2), ch(it, k + 1), ch(it, k), ch(it, k - 1), ch(it, k + 3))
            for i in range(looped, NC):
                if layer == 0 and i == NC - 2 and gate is not None:
                    gate(0)
                single(i)
            if layer == 0 and normed is not None:
                normed(ch(0, NC - 1))
            if layer == 1 and last is not None:
                last(ch(0, NC - 1))

        @block.sync
        def _(sp):
            def weight(n, arrived):
                name = NAMES[n]
                if name in w_src:
                    sp.dma_start(w_nat[:, n, :], w_src[name]).then_inc(arrived, 16)
                else:
                    sp.dma_start(w_nat[:, n, :].rearrange("o (e r) -> o e r", e=E),
                                 u_src[name].rearrange("e o r -> o e r")).then_inc(arrived, 16)

            def vectors():
                sp.dma_start(gw1_nat[:], gw1).then_inc(d_vec, 16)
                sp.dma_start(vb_bc[:], vb[None, :].broadcast_to([128, D])).then_inc(d_vec, 16)
                sp.dma_start(ob_bc[:], ob[None, :].broadcast_to([128, D])).then_inc(d_vec, 16)
                sp.dma_start(qb_c[:], qb[:, None]).then_inc(d_vec, 16)
                sp.dma_start(kb_c[:], kb[:, None]).then_inc(d_vec, 16)
                for j, s_ in enumerate((qS, kS, vS, oS)):
                    sp.dma_start(s_col[:, j:j + 1], s_.rearrange("e r -> (e r)")[:, None]).then_inc(d_vec, 16)
                sp.dma_start(gb1_c[:], gb1[:, None]).then_inc(d_vec, 16)
                sp.dma_start(gw2T[0:GH, :], gw2.rearrange("e g -> g e"), allow_slow_non_contiguous=True).then_inc(d_vec, 16)
                sp.dma_start(gw2T[GH:GH + 1, :], gb2[None, :]).then_inc(d_vec, 16)

            def held(*values):
                return [v if isinstance(v, int) else sp.snap(sp.to_reg(v)) for v in values]

            def load(c):
                came, turned = held(c.u * 16, c.n - 1)
                if after(came):
                    sp.wait_ge(d_x[c.k], came)
                sp.dma_start(x1[:, bass.ds(c.c * NP, NP), :], x_d[:, bass.ds(c.c * NP, NP), :]).then_inc(d_x[c.k], 16)
                if after(turned):
                    sp.wait_ge(cT_ps, turned)
                sp.dma_start(ctx_sb[c.k][:], c_d[:, bass.ds(c.c * NP, NP), :]).then_inc(d_ctx[c.k], 16)

            def put_q(c):
                cut, read = held(c.n + 1, c.u * 16)
                sp.wait_ge(q_lo, cut)
                if after(read):
                    sp.wait_ge(d_qget[c.k], read)
                slots = qpd[c.k].rearrange("h d s t -> (h d) s t")
                sp.dma_start(slots[:, 0:4, :].rearrange("f (r s) t -> f r (s t)", r=2),
                             qpart[c.k][:, 0:2, :].rearrange("f s (r t) -> f r (s t)", r=1).broadcast_to([128, 2, 2 * TOK])
                             ).then_inc(d_qput[c.k], 16)
                sp.dma_start(slots[:, 4:6, :], qpart[c.k][:, 0:3:2, :]).then_inc(d_qput[c.k], 16)

            def put_k(c):
                cut, read = held(c.n + 1, c.u * 32)
                sp.wait_ge(k_lo, cut)
                if after(read):
                    sp.wait_ge(d_kget[c.k], read)
                slots = kpd[c.k].rearrange("h d s t -> (h d) s t")
                sp.dma_start(slots[:, 0:6:2, :], kpart[c.k][:]).then_inc(d_kput[c.k], 16)
                sp.dma_start(slots[:, 1:5:2, :], kpart[c.k][:, 1:3, :]).then_inc(d_kput[c.k], 16)
                sp.dma_start(slots[:, 5, :], kpart[c.k][:, 2, :]).then_inc(d_kput[c.k], 16)

            def put(c):
                if c.layer == 0:
                    put_k(c)
                    put_q(c)
                else:
                    put_q(c)
                    put_k(c)

            def get(c):
                freed, q_stored, k_stored = held((c.n - 1) * 8, c.u * 32 + 32, c.u * 48 + 48)
                if after(freed):
                    sp.wait_ge(s2_ps, freed)

                def get_q():
                    sp.wait_ge(d_qput[c.k], q_stored)
                    sp.dma_start(qst[c.k][:].rearrange("r h p t -> r h (p t)"),
                                 qpd[c.k].rearrange("h d s (b t) -> (d s b) h t", b=2)).then_inc(d_qget[c.k], 16)

                def get_k():
                    sp.wait_ge(d_kput[c.k], k_stored)
                    for b in range(2):
                        sp.dma_start(kbd[c.k][b:ROWS:2, :, S * b:S * b + S, :].rearrange("r h t p -> r h (t p)"),
                                     kpd[c.k].rearrange("h d s (b t) -> b (d s) h t", b=2)[b]).then_inc(d_kget[c.k], 16)
                if c.layer == 0:
                    get_k()
                    get_q()
                else:
                    get_q()
                    get_k()

            for layer in range(2):
                def first(ch):
                    load(ch(0, 0))
                    for n in range(3):
                        weight(n, d_w3)
                    load(ch(0, 1))
                    for n in range(3, NW):
                        weight(n, d_w)
                    put(ch(0, 0))
                    load(ch(0, 2))
                    for j in range(2):
                        if j == 1:
                            vectors()
                            put(ch(0, 1))
                        sp.wait_ge(c_kbd, j + 1)
                        get(ch(0, j))

                def step(prep, mxc, att_c, done, ahead):
                    if ahead is not None and ahead.layer == 0:
                        load(ahead)
                    if prep is not None:
                        put(prep)
                    if prep is not None:
                        get(prep)
                    if done is not None and done.layer == 1:
                        store(done)

                def store(c):
                    ready, at = held(c.c + 1, c.c * NP)
                    sp.wait_ge(o_ok, ready)
                    sp.dma_start(o_d[:, bass.ds(at, NP), :], osb[c.k][:]).then_inc(d_out[c.k], 16)
                walk(sp, layer, step, first=first if layer == 0 else None, last=store)
            for k in range(2):
                sp.wait_ge(d_out[k], 16 * NC // 2)

        @block.gpsimd
        def _(pool):
            nc.gpsimd.memset(ident[:], 0.0).then_inc(c_set, 1)
            nc.gpsimd.memset(m_half[:], -0.5).then_inc(c_set, 1)
            nc.gpsimd.memset(eps_c[:], EPS).then_inc(c_set, 1)
            nc.gpsimd.memset(m_one[:], -1.0).then_inc(c_set, 1)
            pool.wait_ge(c_set, 4)
            nc.gpsimd.affine_select(out=ident[:], in_=ident[:], compare_op=ALU.not_equal, fill=1.0, base=0,
                                    pattern=[[-1, 128]], channel_multiplier=1).then_inc(c_set, 1)
            pool.wait_ge(c_set, 5)

            def constants():
                nc.gpsimd.tensor_copy(identb[:], ident[:]).then_inc(c_tri, 1)
                nc.gpsimd.memset(tri[:], 1.0).then_inc(c_tri, 1)
                pool.wait_ge(c_tri, 2)
                nc.gpsimd.affine_select(out=tri[:], in_=tri[:], compare_op=ALU.is_ge, fill=0.0, base=-1,
                                        pattern=[[1, E], [-1, E]], channel_multiplier=0).then_inc(c_tri, 1)
                pool.wait_ge(c_tri, 3)

            def value_buffers():
                for k in range(2):
                    nc.gpsimd.memset(vbd[k][:], 0.0).then_inc(c_vbd, 1)
                pool.wait_ge(c_vbd, 2)
                for k in range(2):
                    for b in range(2):
                        nc.gpsimd.memset(vbd[k][S * b:S * b + S, :, :, VW * b + DH:VW * b + VW], 1.0).then_inc(c_vbd, 1)
                        pool.wait_ge(c_vbd, 2 * k + b + 3)

            def low_part(c, which):
                mid, rest, part, order, lo = {"q": (q_mid, q_rest, qpart, (1, 2), q_lo),
                                              "k": (k_mid, k_rest, kpart, (1, 0), k_lo)}[which]
                pool.wait_ge(mid, c.n + 1)
                nc.gpsimd.tensor_tensor(part[c.k][:, order[1], :], rest[:], part[c.k][:, order[0], :],
                                        ALU.subtract).then_inc(lo, 1)

            def low_parts(c):
                for which in ("kq", "qk")[c.layer]:
                    low_part(c, which)

            def ahead_rstd(c):
                pool.wait_ge(ln_mv, c.c * NP + NP)
                if after(c.c * NP):
                    pool.wait_ge(ln_x, c.c * NP)
                nc.gpsimd.tensor_tensor(rstd[:], mv[:, :, 1], eps_c[:], ALU.add).then_inc(ln_ve, 1)
                pool.wait_ge(ln_ve, c.c * 3 + 1)
                nc.gpsimd.tensor_tensor(rstd[:], rstd[:], m_half[:], ALU.pow).then_inc(ln_ve, 1)
                pool.wait_ge(ln_ve, c.c * 3 + 2)
                nc.gpsimd.tensor_tensor(shift[:], mv[:, :, 0], rstd[:], ALU.mult).then_inc(ln_ve, 1)
                pool.wait_ge(ln_ve, c.c * 3 + 3)
                nc.gpsimd.tensor_tensor(shift[:], shift[:], m_one[:], ALU.mult).then_inc(ln_rs, 1)

            def result_rstd(c):
                pool.wait_ge(l2_mv, c.c * NP + NP)
                if after(c.c * NP):
                    pool.wait_ge(l2_z, c.c * NP)
                nc.gpsimd.tensor_tensor(rstd2[:], mv2[:, :, 1], eps_c[:], ALU.add).then_inc(l2_ve, 1)
                pool.wait_ge(l2_ve, c.c * 3 + 1)
                nc.gpsimd.tensor_tensor(rstd2[:], rstd2[:], m_half[:], ALU.pow).then_inc(l2_ve, 1)
                pool.wait_ge(l2_ve, c.c * 3 + 2)
                nc.gpsimd.tensor_tensor(shift2[:], mv2[:, :, 0], rstd2[:], ALU.mult).then_inc(l2_ve, 1)
                pool.wait_ge(l2_ve, c.c * 3 + 3)
                nc.gpsimd.tensor_tensor(shift2[:], shift2[:], m_one[:], ALU.mult).then_inc(l2_rs, 1)

            def residual(c, pairs):
                for p in pairs:
                    pool.wait_ge(att_ok, c.n * NP + (p + 1))
                    xp = x1[:, bass.ds(c.c * NP + p, 1), :]
                    nc.gpsimd.tensor_tensor(xp, xp, att[c.k][:, p:p + 1, :], ALU.add).then_inc(add_ok, 1)

            def fetch(c):
                pool.wait_ge(v_ps, c.n)
                pool.wait_ge(zT_ok, c.c + 1)
                nc.gpsimd.tensor_copy(cT[:], zT[:, bass.ds(c.c * TOK, TOK)]).then_inc(f_ok, 1)

            for layer in range(2):
                def first(ch):
                    ahead_rstd(ch(0, 0))
                    constants()
                    value_buffers()
                    ahead_rstd(ch(0, 1))
                    for j in range(2):
                        low_parts(ch(0, j))
                    ahead_rstd(ch(0, 2))

                def step(prep, mxc, att_c, done, ahead):
                    if done is not None and done.layer == 0:
                        result_rstd(done)
                    if prep is not None:
                        low_parts(prep)
                    if done is not None and done.layer == 1:
                        if after(done.c):
                            pool.wait_ge(o_ok, done.c)
                        else:
                            pool.wait_ge(zT_ok, NC)
                        nc.gpsimd.tensor_tensor(xo[:], x1[:, bass.ds(done.c * NP, NP), :],
                                                ob_bc[:, None, :].broadcast_to([128, NP, D]), ALU.add).then_inc(xo_ok, 1)
                    if ahead is not None and ahead.layer == 0:
                        ahead_rstd(ahead)
                    if layer == 0:
                        residual(att_c, (0, 1, 2))
                    if ahead is not None and ahead.layer == 1:
                        fetch(ahead)
                    if layer == 0:
                        residual(att_c, (3,))

                def last(c):
                    pool.wait_ge(o_ok, c.c)
                    nc.gpsimd.tensor_tensor(xo[:], x1[:, bass.ds(c.c * NP, NP), :],
                                            ob_bc[:, None, :].broadcast_to([128, NP, D]), ALU.add).then_inc(xo_ok, 1)
                walk(pool, layer, step, first=first if layer == 0 else None, normed=result_rstd, last=last)

        @block.scalar
        def _(act):
            def weights(names):
                for n in names:
                    act.wait_ge(w_ps, n + 1)
                    nc.scalar.activation(wT[:, n, :], pa[n % 2][:, 0:128], ACT.Copy,
                                         scale=SCALE if NAMES[n] in SCALED else 1.0).then_inc(w_done, 1)

            def ctx_turned(c):
                act.wait_ge(cT_ps, c.n + 1)
                nc.scalar.copy(cT[:], pa[1][:]).then_inc(cT_ok, 1)

            def x_turned(c):
                act.wait_ge(xT_ps, c.n + 1)
                nc.scalar.copy(fT[:], pa[0][:]).then_inc(xT_ok, 1)

            def att_turned(c):
                act.wait_ge(aT_ps, c.c + 1)
                nc.scalar.copy(attT[:], pa[1][:]).then_inc(aT_ok, 1)

            def z_turned(c):
                act.wait_ge(zT_ps, c.c + 1)
                nc.scalar.copy(zT[:, bass.ds(c.c * TOK, TOK)], pa[1][:]).then_inc(zT_ok, 1)

            def first_part(c, which):
                func = ACT.Relu if c.layer == 0 else ACT.Identity
                ps, put, stores, part, at, view, bias, bank, hi = {
                    "q": (q_ps, d_qput, 32, qpart, 0, "f (b p t) -> f p b t", qbs_c, pa[c.layer], q_hi),
                    "k": (k_ps, d_kput, 48, kpart, 2, "f (b t p) -> f p b t", kb_c, pa[1 - c.layer], k_hi)}[which]
                act.wait_ge(ps, c.n + 1)
                if after(c.u * stores):
                    act.wait_ge(put[c.k], c.u * stores)
                nc.scalar.activation(part[c.k][:, at, :].rearrange(view, b=2, p=NP),
                                     bank[:].rearrange("f (p b t) -> f p b t", p=NP, b=2), func,
                                     bias=bias[:] if c.layer else 0.0).then_inc(hi, 1)

            def second_part(c, which):
                rs, rest, part, mid = {"q": (q_r, q_rest, qpart, q_mid), "k": (k_r, k_rest, kpart, k_mid)}[which]
                act.wait_ge(rs, c.n + 1)
                nc.scalar.copy(part[c.k][:, 1, :], rest[:]).then_inc(mid, 1)

            def ahead_apply(c):
                act.wait_ge(ln_rs, c.c + 1)
                if after(c.c - 1):
                    act.wait_ge(xT_ps, c.c - 1)
                for p in range(NP):
                    nc.scalar.activation(xn[c.k][:, p:p + 1, :], x1[:, bass.ds(c.c * NP + p, 1), :], ACT.Identity,
                                         scale=rstd[:, p:p + 1], bias=shift[:, p:p + 1]).then_inc(ln_x, 1)

            def result_apply(c):
                act.wait_ge(l2_rs, c.c + 1)
                if after(c.c):
                    act.wait_ge(zT_ps, c.c)
                for p in range(NP):
                    nc.scalar.activation(z[:, p:p + 1, :], x1[:, bass.ds(c.c * NP + p, 1), :], ACT.Identity,
                                         scale=rstd2[:, p:p + 1], bias=shift2[:, p:p + 1]).then_inc(l2_z, 1)

            def values(c):
                if c.layer == 0:
                    act.wait_ge(v_ps, c.n + 1)
                    if after((c.n - 1) * 8):
                        act.wait_ge(av_ps, (c.n - 1) * 8)
                    for b in range(2):
                        last = nc.scalar.activation(
                            vbd[c.k][S * b:S * b + S, :, :, VW * b:VW * b + DH].rearrange("t p h d -> t (p h) d"),
                            pa[0][S * b:S * b + S, :].rearrange("t (p d) -> t p d", d=DH), ACT.Relu)
                    last.then_inc(v_ok, 1)

            def maxT(c):
                act.wait_ge(mT_pe, c.n + 1)
                if after((c.n - 1) * 8):
                    act.wait_ge(s2_ps, (c.n - 1) * 8)
                nc.scalar.copy(mxT[c.k][:], mT_ps[0:96]).then_inc(mT_ok, 1)

            for layer in range(2):
                def first(ch):
                    ahead_apply(ch(0, 0))
                    weights(range(3))
                    for j in range(2):
                        c = ch(0, j)
                        ctx_turned(c)
                        x_turned(c)
                        first_part(c, "k")
                        first_part(c, "q")
                        second_part(c, "k")
                        second_part(c, "q")
                        if j == 0:
                            ahead_apply(ch(0, 1))
                            act.wait_ge(c_vbd, 6)
                        values(c)
                    weights(range(3, NW))
                    act.wait_ge(w_ps, NW + 1)
                    nc.scalar.activation(gw1T[:], pa[NW % 2][:, 0:GH], ACT.Copy, scale=1.0 / S).then_inc(w_done, 1)
                    act.wait_ge(d_vec, 12 * 16)
                    nc.scalar.mul(qbs_c[:], qb_c[:], SCALE).then_inc(w_done, 1)
                    ahead_apply(ch(0, 2))
                    maxT(ch(0, 0))

                def step(prep, mxc, att_c, done, ahead):
                    g = att_c.n * 8
                    if prep is not None and prep.layer == 0:
                        ctx_turned(prep)
                    for n in range(9):
                        if n < 8:
                            act.wait_ge(s2_ps, g + (n + 1))
                            if after(g + (n - 3)):
                                act.wait_ge(av_ps, g + (n - 3))
                            nc.scalar.activation(prob[n % 4][:].rearrange("p h t -> p (h t)"), s2[n % 2][:],
                                                 ACT.Exp).then_inc(exp_ok, 1)
                        if prep is not None:
                            if n == 1:
                                if prep.layer == 0:
                                    x_turned(prep)
                                first_part(prep, "kq"[prep.layer])
                            if n == 2:
                                first_part(prep, "qk"[prep.layer])
                            if n == 3:
                                second_part(prep, "kq"[prep.layer])
                            if n == 4:
                                second_part(prep, "qk"[prep.layer])
                        if n == 3 and done is not None and done.layer == 0:
                            result_apply(done)
                        if n == 4 and done is not None and done.layer == 1:
                            att_turned(done)
                        if n == MAX_T[layer] and mxc is not None:
                            maxT(mxc)
                        if n == 7 and done is not None and done.layer == 0:
                            z_turned(done)
                        if n >= 2 and n % 2 == 0:
                            p = n // 2 - 1
                            act.wait_ge(av_ps, g + (2 * p + 2))
                            if after(att_c.n * NP + (p - 1)):
                                act.wait_ge(avT_ps, att_c.n * NP + (p - 1))
                            nc.scalar.copy(av_sb[p % 2][:], av[p % 2][:, 0:256]).then_inc(av_ok, 1)
                        if n == 8 and ahead is not None and ahead.layer == 0:
                            ahead_apply(ahead)
                    if prep is not None:
                        values(prep)

                def gate(run):
                    act.wait_ge(g_pe, 1 + 3 * run)
                    nc.scalar.activation(hid[0:GH, :], s1[0][0:GH, 0:B], ACT.Relu, bias=gb1_c[:]).then_inc(g_act, 1)
                    act.wait_ge(g_dve, 4 + 15 * run)
                    nc.scalar.activation(ex[:], lg[:], ACT.Exp, bias=nmax[:]).then_inc(g_act, 1)
                walk(act, layer, step, first=first if layer == 0 else None, gate=gate, normed=result_apply,
                     turned=z_turned, last=att_turned)

        @block.vector
        def _(dve):
            def clear_stack(k):
                nc.vector.memset(kbd[k][:].rearrange("r h t p -> r (h t p)").bitcast(f32), 0.0).then_inc(c_kbd, 1)

            def clear_av():
                for k in range(2):
                    nc.vector.memset(av[k][:], 0.0).then_inc(c_av, 1)
                nc.vector.memset(hid[GH:GH + 1, :], 1.0).then_inc(c_av, 1)

            def ahead_stats(c):
                dve.wait_ge(d_x[c.k], c.u * 16 + 16)
                if after(c.c):
                    dve.wait_ge(ln_rs, c.c)
                for p in range(NP):
                    nc.vector.bn_stats(stats[:, p, :], x1[:, bass.ds(c.c * NP + p, 1), :])
                dve.drain()
                for p in range(NP):
                    nc.vector.bn_aggr(mv[:, p, :], stats[:, p, :]).then_inc(ln_mv, 1)

            def result_stats(c):
                dve.wait_ge(add_ok, c.c * NP + NP)
                if after(c.c):
                    dve.wait_ge(l2_rs, c.c)
                for p in range(NP):
                    nc.vector.bn_stats(stats2[:, p, :], x1[:, bass.ds(c.c * NP + p, 1), :])
                dve.drain()
                for p in range(NP):
                    nc.vector.bn_aggr(mv2[:, p, :], stats2[:, p, :]).then_inc(l2_mv, 1)

            def pool_tokens(c):
                dve.wait_ge(zT_ok, c.c + 1)
                nc.vector.tensor_reduce(pooled[:, bass.ds(c.c * 2 * NP, 2 * NP)],
                                        zT[:, bass.ds(c.c * TOK, TOK)].rearrange("f (b t) -> f b t", t=S),
                                        AX.X, ALU.add).then_inc(pool_ok, 1)

            def rest(c, which):
                if which == "q":
                    ps, hi, rs, lo, part, first, dst, bias, view = (
                        pa[c.layer], q_hi, q_r, q_lo, qpart, 0, q_rest, qbs_c, "f (b p t) -> f p b t")
                else:
                    ps, hi, rs, lo, part, first, dst, bias, view = (
                        pa[1 - c.layer], k_hi, k_r, k_lo, kpart, 2, k_rest, kb_c, "f (b t p) -> f p b t")
                dve.wait_ge(hi, c.n + 1)
                if after(c.n):
                    dve.wait_ge(lo, c.n)
                for b in range(2):
                    last = nc.vector.scalar_tensor_tensor(out=dst[:].rearrange(view, b=2, p=NP)[:, :, b],
                                                          in0=ps[:].rearrange("f (p b t) -> f p b t", p=NP, b=2)[:, :, b],
                                                          scalar=bias[:] if c.layer else 0.0,
                                                          in1=part[c.k][:, first, :].rearrange(view, b=2, p=NP)[:, :, b],
                                                          op0=ALU.add if c.layer else ALU.max, op1=ALU.subtract)
                last.then_inc(rs, 1)

            def gate_rank(c, p, bank):
                dve.wait_ge(xv_ps[p], c.c + 1)
                if p == "v" or p == "q" or p == "k":
                    used = {"q": q_ps, "k": k_ps, "v": v_ps}[p]
                    if after(c.c):
                        dve.wait_ge(used, c.n)
                elif after(c.c):
                    dve.wait_ge(o_ps, c.c)
                nc.vector.tensor_tensor(xvs[p][:].rearrange("e (b t) -> e b t", t=S), bank[:].rearrange("e (b t) -> e b t", t=S),
                                        sg[p][:, bass.ds(c.c * 2 * NP, 2 * NP)].rearrange("e (b o) -> e b o", o=1).broadcast_to([128, 2 * NP, S]),
                                        ALU.mult).then_inc(xv_ok[p], 1)

            def maxima(c, unit):
                p, g = unit // 2, unit % 2
                dve.wait_ge(sc_ps, c.n * 8 + (unit + 1))
                nc.vector.tensor_reduce(mx[:, 2 * g:2 * g + 2, :].rearrange("q b (g p) -> q g b p", p=NP)[:, :, :, p],
                                        s1[unit % 2][:].rearrange("q (g b k) -> q g b k", g=4, b=2),
                                        AX.X, ALU.max).then_inc(max_ok, 1)

            def max_parts(c):
                dve.wait_ge(max_ok, c.n * 8 + 8)
                if after(c.n):
                    dve.wait_ge(mT_pe, c.n)
                nc.vector.tensor_scalar(mxp[:, :, 0, :], mx[:], -1.0, None, ALU.mult).then_inc(m_hi, 1)
                dve.wait_ge(m_hi, c.n + 1)
                nc.vector.scalar_tensor_tensor(out=mx_rest[:], in0=mx[:], scalar=-1.0, in1=mxp[:, :, 0, :],
                                               op0=ALU.mult, op1=ALU.subtract).then_inc(m_r, 1)
                dve.wait_ge(m_r, c.n + 1)
                nc.vector.tensor_copy(mxp[:, :, 1, :], mx_rest[:]).then_inc(m_mid, 1)
                dve.wait_ge(m_mid, c.n + 1)
                nc.vector.tensor_tensor(mxp[:, :, 2, :], mx_rest[:], mxp[:, :, 1, :], ALU.subtract).then_inc(m_parts, 1)

            def divide(c, p):
                j = c.n * NP + (p + 1)
                dve.wait_ge(avT_ps, j)
                vw = av[p % 2][:, 256:512].rearrange("q (g w) -> q g w", w=32)
                nc.vector.reciprocal(rden[:, p % 2], vw[:, :, DH:2 * VW:VW]).then_inc(rden_ok, 1)
                dve.wait_ge(rden_ok, j)
                if c.layer == 0 and after((c.n - 2) * NP + (p + 1)):
                    dve.wait_ge(add_ok, (c.n - 2) * NP + (p + 1))
                if c.layer == 1 and after(c.c - 1):
                    dve.wait_ge(aT_ps, c.c - 1)
                for hp in range(2):
                    for b in range(2):
                        q0 = S * hp
                        last = nc.vector.tensor_tensor(
                            att[c.k][S * b:S * b + S, p, :].rearrange("q (s e c d) -> q s e c d", s=2, e=2, c=4)[:, :, hp],
                            vw[q0:q0 + S, :, VW * b:VW * b + DH].rearrange("q (s c) d -> q s c d", s=2),
                            rden[q0:q0 + S, p % 2, :, b:b + 1].rearrange("q (s c) o -> q s c o", s=2).broadcast_to([S, 2, 4, DH]), ALU.mult)
                last.then_inc(att_ok, 1)

            def values(c):
                if c.layer == 1:
                    dve.wait_ge(v_ps, c.n + 1)
                    if after((c.n - 1) * 8):
                        dve.wait_ge(av_ps, (c.n - 1) * 8)
                    for b in range(2):
                        last = nc.vector.tensor_tensor(
                            vbd[c.k][S * b:S * b + S, :, :, VW * b:VW * b + DH],
                            pa[0][S * b:S * b + S, :].rearrange("t (p h d) -> t p h d", p=NP, h=H),
                            vb_bc[S * b:S * b + S, :].rearrange("t (o h d) -> t o h d", o=1, h=H).broadcast_to([S, NP, H, DH]), ALU.add)
                    last.then_inc(v_ok, 1)

            def result(c):
                dve.wait_ge(o_ps, c.c + 1)
                dve.wait_ge(xo_ok, c.c + 1)
                if after((c.c - 1)):
                    dve.wait_ge(d_out[c.k], (c.u - NC // 2) * 16)
                nc.vector.tensor_tensor(osb[c.k][:].rearrange("t p f -> t (p f)"), pa[1][:],
                                        xo[:].rearrange("t p f -> t (p f)"), ALU.add).then_inc(o_ok, 1)

            for layer in range(2):
                def first(ch):
                    ahead_stats(ch(0, 0))
                    clear_stack(0)
                    ahead_stats(ch(0, 1))
                    for j in range(2):
                        rest(ch(0, j), "k")
                        rest(ch(0, j), "q")
                        if j == 0:
                            clear_stack(1)
                    clear_av()
                    nc.vector.memset(pooled[:], 0.0)
                    dve.wait_ge(c_set, 5)
                    nc.vector.tensor_reduce(pick_of[:], ident[0:2 * PARTS * GP, 0:2 * PARTS * GP].rearrange(
                        "r (b s i) -> r b i s", b=2, s=PARTS), AX.X, ALU.add).then_inc(c_pick, 1)
                    dve.wait_ge(c_pick, 1)
                    nc.vector.tensor_copy(pick[:].rearrange("r i (b t) -> r i b t", b=2),
                                          pick_of[:].rearrange("r b (i o) -> r i b o", o=1).broadcast_to(
                                              [2 * PARTS * GP, GP, 2, S])).then_inc(c_pick, 1)
                    ahead_stats(ch(0, 2))
                    for u in range(8):
                        maxima(ch(0, 0), u)
                    max_parts(ch(0, 0))

                def step(prep, mxc, att_c, done, ahead):
                    for n in range(10):
                        if mxc is not None:
                            for unit in UNITS[layer].get(n, ()):
                                maxima(mxc, unit)
                            if n == LAST_UNITS[layer]:
                                max_parts(mxc)
                        if n == 0 and done is not None and done.layer == 0:
                            result_stats(done)
                        if prep is not None:
                            if n == 0 and prep.layer == 1:
                                gate_rank(prep, "q", pa[1])
                                gate_rank(prep, "k", pa[0])
                            if n == 1:
                                rest(prep, "kq"[prep.layer])
                            if n == 2:
                                rest(prep, "qk"[prep.layer])
                            if n == 5 and prep.layer == 1:
                                gate_rank(prep, "v", pa[0])
                            if n == 9 and prep.layer == 1:
                                values(prep)
                        if n == 4 and done is not None and done.layer == 1:
                            gate_rank(done, "o", pa[1])
                        if n == 5 and ahead is not None and ahead.layer == 0:
                            ahead_stats(ahead)
                        if n == 7 and done is not None and done.layer == 1:
                            result(done)
                        if n == 8 and done is not None and done.layer == 0:
                            pool_tokens(done)
                        if n >= 3 and n % 2 == 1:
                            divide(att_c, (n - 3) // 2)

                def last(c):
                    gate_rank(c, "o", pa[1])
                    result(c)

                def gate(run):
                    dve.wait_ge(g_pe, 2 + 3 * run)
                    nc.vector.tensor_copy(lg[:], s1[1][:, 0:E]).then_inc(g_dve, 1)
                    dve.wait_ge(g_dve, 1 + 15 * run)
                    dve.wait_ge(c_tri, 3)
                    dve.wait_ge(d_vec, 12 * 16)
                    other = lg[:].rearrange("b (o e) -> b o e", o=1).broadcast_to([128, E, E])
                    own = lg[:].rearrange("b (e o) -> b e o", o=1).broadcast_to([128, E, E])
                    nc.vector.tensor_tensor(beat[:], other, own, ALU.is_gt).then_inc(g_dve, 1)
                    nc.vector.tensor_tensor(tie[:], other, own, ALU.is_equal).then_inc(g_dve, 1)
                    nc.vector.tensor_reduce(nmax[:], lg[:], AX.X, ALU.max, negate=True).then_inc(g_dve, 1)
                    dve.wait_ge(g_dve, 4 + 15 * run)
                    nc.vector.tensor_tensor(tie[:], tie[:], tri[:], ALU.mult).then_inc(g_dve, 1)
                    dve.wait_ge(g_dve, 5 + 15 * run)
                    nc.vector.tensor_tensor(beat[:], beat[:], tie[:], ALU.add).then_inc(g_dve, 1)
                    dve.wait_ge(g_dve, 6 + 15 * run)
                    nc.vector.tensor_reduce(rank[:], beat[:], AX.X, ALU.add).then_inc(g_dve, 1)
                    dve.wait_ge(g_dve, 7 + 15 * run)
                    dve.wait_ge(g_act, 2 + 2 * run)
                    nc.vector.scalar_tensor_tensor(out=ex[:], in0=rank[:], scalar=1.5, in1=ex[:],
                                                   op0=ALU.is_lt, op1=ALU.mult).then_inc(g_dve, 1)
                    dve.wait_ge(g_dve, 8 + 15 * run)
                    nc.vector.tensor_reduce(gsum[:], ex[:], AX.X, ALU.add).then_inc(g_dve, 1)
                    dve.wait_ge(g_dve, 9 + 15 * run)
                    nc.vector.reciprocal(rsum[:], gsum[:]).then_inc(g_dve, 1)
                    dve.wait_ge(g_dve, 10 + 15 * run)
                    nc.vector.tensor_scalar(gexp[:], ex[:].rearrange("b (e o) -> b e o", o=1).broadcast_to([128, E, R]),
                                            rsum[:], None, ALU.mult).then_inc(g_dve, 1)
                    dve.wait_ge(g_pe, 3 + 3 * run)
                    for j, p in enumerate("qkvo"):
                        nc.vector.tensor_scalar(sg[p][:], s1[0][:, 0:B], s_col[:, j:j + 1], None, ALU.mult).then_inc(g_dve, 1)
                    dve.wait_ge(g_dve, 15 + 15 * run)
                walk(dve, layer, step, first=first if layer == 0 else None, gate=gate, normed=result_stats,
                     turned=pool_tokens, last=last)

        @block.tensor
        def _(pe):
            def turn_weights(names):
                for n in names:
                    if n >= 2 and n != 3:
                        pe.wait_ge(w_done, n - 1)
                    nc.tensor.transpose(pa[n % 2][:, 0:128], w_nat[:, n, :], ident[:]).then_inc(w_ps, 1)

            def W(name):
                return wT[:, WI[name], :]

            def turn_ctx(c):
                pe.wait_ge(d_ctx[c.k], c.u * 16 + 16)
                if after(c.n):
                    pe.wait_ge(k_r, c.n)
                if after(c.c - 3):
                    pe.wait_ge(zT_ok, c.c - 3)
                for p in range(NP):
                    last = nc.tensor.transpose(pa[1][:, 128 * p:128 * p + 128], ctx_sb[c.k][:, p, :], ident[:])
                last.then_inc(cT_ps, 1)

            def turn_x(c):
                pe.wait_ge(ln_x, c.c * NP + NP)
                if after(c.n):
                    pe.wait_ge(v_ok, c.n)
                for p in range(NP):
                    last = nc.tensor.transpose(pa[0][:, 128 * p:128 * p + 128], xn[c.k][:, p, :], ident[:])
                last.then_inc(xT_ps, 1)

            def cross_keys(c):
                pe.wait_ge(cT_ok, c.c + 1)
                nc.tensor.matmul(pa[1][:], W("wk"), cT[:], start=True, stop=True).then_inc(k_ps, 1)

            def cross_queries(c):
                pe.wait_ge(xT_ok, c.c + 1)
                nc.tensor.matmul(pa[0][:], W("wq"), fT[:], start=True, stop=True).then_inc(q_ps, 1)

            def turn_z(c, prep):
                pe.wait_ge(l2_z, c.c * NP + NP)
                pe.wait_ge(k_r if prep.layer == 0 else q_r, prep.n + 1)
                for p in range(NP):
                    last = nc.tensor.transpose(pa[1][:, 128 * p:128 * p + 128], z[:, p, :], ident[:])
                last.then_inc(zT_ps, 1)

            def query_ranks(c):
                pe.wait_ge(f_ok, c.c + 1)
                if isinstance(c.c, int) and c.c < 4:
                    if c.c == 0:
                        pe.wait_ge(k_r, NC)
                    pe.wait_ge(zT_ok, NC - 3 + c.c)
                pe.wait_ge(q_r, c.n)
                if after(c.c - 3):
                    pe.wait_ge(o_ok, c.c - 3)
                nc.tensor.matmul(pa[1][:], W("qV"), cT[:], start=True, stop=True).then_inc(xv_ps["q"], 1)

            def key_ranks(c):
                pe.wait_ge(v_ok, c.n)
                nc.tensor.matmul(pa[0][:], W("kV"), cT[:], start=True, stop=True).then_inc(xv_ps["k"], 1)

            def project(c, p, bank, done):
                pe.wait_ge(xv_ok[p], c.c + 1)
                nc.tensor.matmul(bank[:], W(p + "W"), cT[:], start=True, stop=False)
                nc.tensor.matmul(bank[:], W(p + "U"), xvs[p][:], start=False, stop=True).then_inc(done, 1)

            def value_ranks(c):
                pe.wait_ge(k_r, c.n + 1)
                nc.tensor.matmul(pa[0][:], W("vV"), cT[:], start=True, stop=True).then_inc(xv_ps["v"], 1)

            def turn_att(c, prep):
                pe.wait_ge(att_ok, c.n * NP + NP)
                if prep is not None:
                    pe.wait_ge(q_r, prep.n + 1)
                else:
                    pe.wait_ge(q_r, 2 * NC)
                    pe.wait_ge(o_ok, c.c)
                for p in range(NP):
                    last = nc.tensor.transpose(pa[1][:, 128 * p:128 * p + 128], att[c.k][:, p, :], ident[:])
                last.then_inc(aT_ps, 1)

            def output_ranks(c):
                pe.wait_ge(aT_ok, c.c + 1)
                nc.tensor.matmul(pa[1][:], W("oV"), attT[:], start=True, stop=True).then_inc(xv_ps["o"], 1)

            def output(c):
                pe.wait_ge(xv_ok["o"], c.c + 1)
                for p in range(NP):
                    cols = slice(128 * p, 128 * p + 128)
                    nc.tensor.matmul(pa[1][:, cols], attT[:, cols], W("oW"), start=True, stop=False)
                    last = nc.tensor.matmul(pa[1][:, cols], xvs["o"][:, cols], W("oU"), start=False, stop=True)
                last.then_inc(o_ps, 1)

            def values(c):
                if c.layer == 0:
                    pe.wait_ge(q_r, c.n + 1)
                else:
                    pe.wait_ge(xv_ok["v"], c.c + 1)
                for p in range(NP):
                    cols = slice(128 * p, 128 * p + 128)
                    if c.layer == 0:
                        last = nc.tensor.matmul(pa[0][:, cols], cT[:, cols], W("wv"), start=True, stop=True)
                    else:
                        nc.tensor.matmul(pa[0][:, cols], cT[:, cols], W("vW"), start=True, stop=False)
                        last = nc.tensor.matmul(pa[0][:, cols], xvs["v"][:, cols], W("vU"), start=False, stop=True)
                last.then_inc(v_ps, 1)

            def scores(c, unit):
                p, g = unit // 2, unit % 2
                if unit == 0:
                    pe.wait_ge(d_qget[c.k], c.u * 16 + 16)
                    pe.wait_ge(d_kget[c.k], c.u * 32 + 32)
                    if after(c.n):
                        pe.wait_ge(mT_ok, c.n)
                if after(c.n * 8 + (unit - 1)):
                    pe.wait_ge(max_ok, c.n * 8 + (unit - 1))
                for j in range(4):
                    for a in range(2):
                        h = 2 * (4 * g + j) + a
                        last = nc.tensor.matmul(s1[unit % 2][S * a:S * a + S, 128 * j:128 * j + 128],
                                                qst[c.k][0:ROWS, h, p, :], kbd[c.k][0:ROWS, h, :, p], start=True, stop=True)
                last.then_inc(sc_ps, 1)

            def maxT(c):
                pe.wait_ge(m_parts, c.n + 1)
                for half in range(2):
                    last = nc.tensor.transpose(mT_ps[0:2 * PARTS * GP, half, :],
                                               mxp[:, 2 * half:2 * half + 2].rearrange("q b s i -> q (b s i)"), identb[:])
                last.then_inc(mT_pe, 1)

            def shifted(c, n):
                p, half = n // 2, n % 2
                if n == 0:
                    pe.wait_ge(mT_ok, c.n + 1)
                if after(c.n * 8 + (n - 1)):
                    pe.wait_ge(exp_ok, c.n * 8 + (n - 1))
                for g in range(UNIT_H // 2):
                    nc.tensor.matmul(s2[n % 2][:, 2 * S * g:2 * S * g + 2 * S], pick[:, NP * g + p, :], mxT[c.k][:, half, :],
                                     start=True, stop=False)
                    for j in range(2 * g, 2 * g + 2):
                        h = UNIT_H * half + j
                        last = nc.tensor.matmul(s2[n % 2][:, S * j:S * j + S], kbd[c.k][:, h, :, p], qst[c.k][:, h, p, :],
                                                start=False, stop=j % 2 == 1)
                last.then_inc(s2_ps, 1)

            def times_values(c, n):
                p, half = n // 2, n % 2
                pe.wait_ge(exp_ok, c.n * 8 + (n + 1))
                if n == 0:
                    pe.wait_ge(v_ok, c.n + 1)
                if half == 0 and after(c.n * NP + (p - 1)):
                    pe.wait_ge(att_ok, c.n * NP + (p - 1))
                for j in range(8):
                    h = 8 * half + j
                    g = h // 4
                    last = nc.tensor.matmul(av[p % 2][32 * (h % 4):32 * (h % 4) + 2 * VW, S * g:S * g + S],
                                            vbd[c.k][:, p, h, :], prob[n % 4][:, j, :], start=True, stop=True)
                last.then_inc(av_ps, 1)

            def turn(c, p):
                pe.wait_ge(av_ok, c.n * NP + (p + 1))
                for s in range(2):
                    last = nc.tensor.transpose(av[p % 2][:, 256 + 128 * s:384 + 128 * s],
                                               av_sb[p % 2][:, 128 * s:128 * s + 128], ident[:])
                last.then_inc(avT_ps, 1)

            for layer in range(2):
                def first(ch):
                    pe.wait_ge(c_set, 5)
                    pe.wait_ge(d_w3, 48)
                    turn_weights(range(3))
                    pe.wait_ge(w_done, 3)
                    for j in range(2):
                        c = ch(0, j)
                        turn_ctx(c)
                        turn_x(c)
                        cross_keys(c)
                        cross_queries(c)
                        values(c)
                    pe.wait_ge(v_ok, 2)
                    pe.wait_ge(k_r, 2)
                    pe.wait_ge(d_w, 16 * (NW - 3))
                    pe.wait_ge(c_tri, 1)
                    for u in range(8):
                        if u < 6:
                            turn_weights(range(3 + 2 * u, 5 + 2 * u))
                        scores(ch(0, 0), u)
                    pe.wait_ge(w_done, NW - 1)
                    pe.wait_ge(d_vec, 12 * 16)
                    nc.tensor.transpose(pa[NW % 2][:, 0:GH], gw1_nat[:], ident[0:GH, 0:GH]).then_inc(w_ps, 1)
                    maxT(ch(0, 0))
                    pe.wait_ge(w_done, NW + 2)
                    pe.wait_ge(c_av, 2)
                    pe.wait_ge(c_pick, 2)

                def step(prep, mxc, att_c, done, ahead):
                    if prep is not None and prep.layer == 0:
                        turn_ctx(prep)
                    for n in range(10):
                        if n < 8:
                            shifted(att_c, n)
                        if prep is not None:
                            if n == 0 and prep.layer == 1:
                                query_ranks(prep)
                                key_ranks(prep)
                            if n == 1:
                                if prep.layer == 0:
                                    turn_x(prep)
                                    cross_keys(prep)
                                else:
                                    project(prep, "q", pa[1], q_ps)
                            if n == 2:
                                if prep.layer == 0:
                                    cross_queries(prep)
                                else:
                                    project(prep, "k", pa[0], k_ps)
                        if mxc is not None:
                            for unit in UNITS[layer].get(n, ()):
                                scores(mxc, unit)
                        if n == MAX_T[layer] and mxc is not None:
                            maxT(mxc)
                        if n == 7 and done is not None and done.layer == 0:
                            turn_z(done, prep)
                        if n == 4 and prep is not None and prep.layer == 1:
                            value_ranks(prep)
                        if 1 <= n <= 8:
                            times_values(att_c, n - 1)
                        if done is not None and done.layer == 1:
                            if n == 3:
                                turn_att(done, prep)
                            if n == 4:
                                output_ranks(done)
                            if n == 6:
                                output(done)
                        if prep is not None and n == (9, 6)[prep.layer]:
                            values(prep)
                        if n >= 3 and n % 2 == 1:
                            turn(att_c, (n - 3) // 2)

                def last(c):
                    turn_att(c, None)
                    output_ranks(c)
                    output(c)

                def gate(run):
                    pe.wait_ge(pool_ok, (NC - 3, NC)[run])
                    pe.wait_ge(c_av, 3)
                    pe.wait_ge(mT_ok, NC - 1 + 3 * run)
                    pe.wait_ge(max_ok, 8 * (NC - 1 + 3 * run))
                    nc.tensor.matmul(s1[0][0:GH, 0:B], gw1T[:], pooled[:], start=True, stop=True).then_inc(g_pe, 1)
                    pe.wait_ge(g_act, 1 + 2 * run)
                    nc.tensor.matmul(s1[1][:, 0:E], hid[:], gw2T[:], start=True, stop=True).then_inc(g_pe, 1)
                    pe.wait_ge(g_dve, 11 + 15 * run)
                    nc.tensor.transpose(s1[0][:, 0:B], gexp[:].rearrange("b e r -> b (e r)"), ident[:]).then_inc(g_pe, 1)
                    pe.wait_ge(g_dve, 15 + 15 * run)
                walk(pe, layer, step, first=first if layer == 0 else None, gate=gate,
                     turned=lambda c: turn_z(c, Chunk(1, 0, 2)), last=last)


_P = ("Wm", "U", "S", "V", "b")
_INS = (["x", "ctx_1024", "L0_xattn_Wq", "L0_xattn_Wk", "L0_xattn_Wv",
         "L0_ffn_gw1", "L0_ffn_gb1", "L0_ffn_gw2", "L0_ffn_gb2"]
        + ["L0_ffn_" + p + s for p in "qkvo" for s in _P])
_OUTS = [((B, S, D), 'float32')]


def kernel(**inputs):
    import numpy as _np
    import concourse.bacc as _bacc
    from concourse import mybir as _mybir
    from concourse.bass_utils import run_bass_kernel_spmd as _run

    nc = _bacc.Bacc("TRN2", target_bir_lowering=False, num_devices=1)
    arrays, args = {}, []
    for name in _INS:
        a = _np.ascontiguousarray(inputs[name])
        arrays[f"in_{name}_dram"] = a
        args.append(nc.dram_tensor(f"in_{name}_dram", a.shape, _mybir.dt.from_np(a.dtype), kind="ExternalInput").ap())
    for i, (shape, dtype) in enumerate(_OUTS):
        dt = _mybir.dt.from_np(_np.dtype(dtype))
        args.append(nc.dram_tensor(f"out_{i}_dram", shape, dt, kind="ExternalOutput").ap())
    xattn_ffn_kernel(nc, *args)
    r = _run(nc, [arrays], core_ids=[0])
    got = tuple(r.results[0][f"out_{i}_dram"] for i in range(len(_OUTS)))
    return got[0]
```
